# Optimizing a Trainium2 kernel written in Bass

```python
import numpy as np
import jax
import jax.numpy as jnp

def _softmax(x, axis=-1):
    return jax.nn.softmax(x, axis=axis)

def _gelu(x):
    return jax.nn.gelu(x, approximate=True)

def _silu(x):
    return jax.nn.silu(x)

def _sigmoid(x):
    return jax.nn.sigmoid(x)

def _layernorm(x, axis=-1, eps=1e-05):
    m = jnp.mean(x, axis=axis, keepdims=True)
    v = jnp.var(x, axis=axis, keepdims=True)
    return (x - m) / jnp.sqrt(v + eps)

def _scatter_add(tgt, idx, src, axis=0):
    return tgt.at[idx].add(src)

def _segment_sum(src, seg, n):
    return jax.ops.segment_sum(src, seg, n)
kernel_name = 'mk_adaln_d1_jaxref_r8_93625d'

def setup_inputs(seed: int=0):
    np.random.seed(seed)
    _w = jnp.asarray

    def _L0_attn_setup():
        import math
        import jax, jax.numpy as jnp
        import numpy as np
        H = 32
        NOPE = 64
        ROPE = 64
        VD = 128
        QHD = NOPE + ROPE
        KVR = 32
        EPS = 1e-06

        def _yarn_cos_sin(seq_len, dim=ROPE, base=10000.0, factor=128.0, beta_fast=32.0, beta_slow=1.0, orig_max=1024, mscale=1.0, mscale_all_dim=1.0):

            def corr_dim(r):
                return dim * math.log(orig_max / (r * 2 * math.pi)) / (2 * math.log(base))
            low = max(math.floor(corr_dim(beta_fast)), 0)
            high = min(math.ceil(corr_dim(beta_slow)), dim - 1)
            hi = high + 0.001 if low == high else float(high)
            ramp = np.clip((np.arange(dim // 2, dtype=np.float32) - low) / (hi - low), 0.0, 1.0)
            inv_freq_mask = 1.0 - ramp
            freq_extra = 1.0 / base ** (np.arange(0, dim, 2, dtype=np.float32) / dim)
            freq_inter = freq_extra / factor
            inv_freq = freq_inter * (1.0 - inv_freq_mask) + freq_extra * inv_freq_mask
            t = np.arange(seq_len, dtype=np.float32)
            freqs = np.outer(t, inv_freq)
            emb = np.concatenate([freqs, freqs], axis=-1)

            def gm(s, m):
                return 1.0 if s <= 1 else 0.1 * m * math.log(s) + 1.0
            ms = gm(factor, mscale) / gm(factor, mscale_all_dim)
            return (jnp.asarray(np.cos(emb) * ms), jnp.asarray(np.sin(emb) * ms))

        def _rmsnorm(x, w, eps=EPS):
            var = jnp.mean(jnp.square(x), axis=-1, keepdims=True)
            return x * jax.lax.rsqrt(var + eps) * w

        def _deinterleave(x):
            d = x.shape[-1]
            x = x.reshape(*x.shape[:-1], d // 2, 2)
            return jnp.concatenate([x[..., 0], x[..., 1]], axis=-1)

        def _rotate_half(x):
            d = x.shape[-1] // 2
            return jnp.concatenate([-x[..., d:], x[..., :d]], axis=-1)

        def _apply_rope(x, cos, sin):
            return x * cos + _rotate_half(x) * sin
        key = jax.random.key(seed)
        ks = jax.random.split(key, 6)
        B, S, D = (1, 256, 512)
        std = 0.02
        return {'x': jax.random.normal(ks[0], (B, S, D), dtype=jnp.float32), 'wq_a': jax.random.normal(ks[1], (128, D), dtype=jnp.float32) * std, 'q_a_ln_w': jnp.ones((128,), dtype=jnp.float32), 'wq_b': jax.random.normal(ks[2], (H * QHD, 128), dtype=jnp.float32) * std, 'wkv_a': jax.random.normal(ks[3], (KVR + ROPE, D), dtype=jnp.float32) * std, 'kv_a_ln_w': jnp.ones((KVR,), dtype=jnp.float32), 'wkv_b': jax.random.normal(ks[4], (H * (NOPE + VD), KVR), dtype=jnp.float32) * std, 'wo': jax.random.normal(ks[5], (D, H * VD), dtype=jnp.float32) * std}
    _L0_attn_in = _L0_attn_setup()

    def _L0_ffn_setup():
        import jax, jax.numpy as jnp
        import numpy as np
        EPS = 1e-05

        def _bitlinear(x, w):
            scale = jnp.mean(jnp.abs(w))
            q = jnp.round(jnp.clip(w / (scale + EPS), -1.0, 1.0))
            deq = q * scale
            return x @ deq.T
        key = jax.random.key(seed)
        k1, k2, k3, k4 = jax.random.split(key, 4)
        B, S, H, I = (4, 256, 512, 1376)
        return {'hidden_states': jax.random.normal(k1, (B, S, H), dtype=jnp.float32), 'w_gate': jax.random.normal(k2, (I, H), dtype=jnp.float32) * 0.02, 'w_up': jax.random.normal(k3, (I, H), dtype=jnp.float32) * 0.02, 'w_down': jax.random.normal(k4, (H, I), dtype=jnp.float32) * 0.02}
    _L0_ffn_in = _L0_ffn_setup()
    _L0_c = _w((lambda *s: np.random.randn(*s).astype(np.float32) * 0.05)(4, 512))
    _L0_wmod = _w((lambda *s: np.random.randn(*s).astype(np.float32) * 0.05)(512, 6 * 512) * 512 ** (-0.5))
    _d = {'L0_attn_x': _L0_attn_in['x'], 'L0_attn_wq_a': _L0_attn_in['wq_a'], 'L0_attn_q_a_ln_w': _L0_attn_in['q_a_ln_w'], 'L0_attn_wq_b': _L0_attn_in['wq_b'], 'L0_attn_wkv_a': _L0_attn_in['wkv_a'], 'L0_attn_kv_a_ln_w': _L0_attn_in['kv_a_ln_w'], 'L0_attn_wkv_b': _L0_attn_in['wkv_b'], 'L0_attn_wo': _L0_attn_in['wo'], 'L0_ffn_w_gate': _L0_ffn_in['w_gate'], 'L0_ffn_w_up': _L0_ffn_in['w_up'], 'L0_ffn_w_down': _L0_ffn_in['w_down'], 'L0_c': _L0_c, 'L0_wmod': _L0_wmod}
    _x0 = _d['L0_attn_x']
    _d['L0_attn_x'] = jax.random.normal(jax.random.fold_in(jax.random.key(seed), 1), (4, 512, 512), dtype=_x0.dtype)
    del _x0
    return _d

def reference(L0_attn_x, L0_attn_wq_a, L0_attn_q_a_ln_w, L0_attn_wq_b, L0_attn_wkv_a, L0_attn_kv_a_ln_w, L0_attn_wkv_b, L0_attn_wo, L0_ffn_w_gate, L0_ffn_w_up, L0_ffn_w_down, L0_c, L0_wmod):

    def _L0_attn_ref(x, wq_a, q_a_ln_w, wq_b, wkv_a, kv_a_ln_w, wkv_b, wo):
        import math
        import jax, jax.numpy as jnp
        import numpy as np
        H = 32
        NOPE = 64
        ROPE = 64
        VD = 128
        QHD = NOPE + ROPE
        KVR = 32
        EPS = 1e-06

        def _yarn_cos_sin(seq_len, dim=ROPE, base=10000.0, factor=128.0, beta_fast=32.0, beta_slow=1.0, orig_max=1024, mscale=1.0, mscale_all_dim=1.0):

            def corr_dim(r):
                return dim * math.log(orig_max / (r * 2 * math.pi)) / (2 * math.log(base))
            low = max(math.floor(corr_dim(beta_fast)), 0)
            high = min(math.ceil(corr_dim(beta_slow)), dim - 1)
            hi = high + 0.001 if low == high else float(high)
            ramp = np.clip((np.arange(dim // 2, dtype=np.float32) - low) / (hi - low), 0.0, 1.0)
            inv_freq_mask = 1.0 - ramp
            freq_extra = 1.0 / base ** (np.arange(0, dim, 2, dtype=np.float32) / dim)
            freq_inter = freq_extra / factor
            inv_freq = freq_inter * (1.0 - inv_freq_mask) + freq_extra * inv_freq_mask
            t = np.arange(seq_len, dtype=np.float32)
            freqs = np.outer(t, inv_freq)
            emb = np.concatenate([freqs, freqs], axis=-1)

            def gm(s, m):
                return 1.0 if s <= 1 else 0.1 * m * math.log(s) + 1.0
            ms = gm(factor, mscale) / gm(factor, mscale_all_dim)
            return (jnp.asarray(np.cos(emb) * ms), jnp.asarray(np.sin(emb) * ms))

        def _rmsnorm(x, w, eps=EPS):
            var = jnp.mean(jnp.square(x), axis=-1, keepdims=True)
            return x * jax.lax.rsqrt(var + eps) * w

        def _deinterleave(x):
            d = x.shape[-1]
            x = x.reshape(*x.shape[:-1], d // 2, 2)
            return jnp.concatenate([x[..., 0], x[..., 1]], axis=-1)

        def _rotate_half(x):
            d = x.shape[-1] // 2
            return jnp.concatenate([-x[..., d:], x[..., :d]], axis=-1)

        def _apply_rope(x, cos, sin):
            return x * cos + _rotate_half(x) * sin
        B, S, D = x.shape
        m = 0.1 * 1.0 * math.log(128.0) + 1.0
        softmax_scale = QHD ** (-0.5) * m * m
        q = _rmsnorm(x @ wq_a.T, q_a_ln_w) @ wq_b.T
        q = q.reshape(B, S, H, QHD)
        q_nope, q_pe = (q[..., :NOPE], q[..., NOPE:])
        ckv_kpe = x @ wkv_a.T
        ckv, k_pe = (ckv_kpe[..., :KVR], ckv_kpe[..., KVR:])
        kv = _rmsnorm(ckv, kv_a_ln_w) @ wkv_b.T
        kv = kv.reshape(B, S, H, NOPE + VD)
        k_nope, v = (kv[..., :NOPE], kv[..., NOPE:])
        cos, sin = _yarn_cos_sin(S)
        q_pe = _apply_rope(_deinterleave(q_pe), cos[None, :, None, :], sin[None, :, None, :])
        k_pe = _apply_rope(_deinterleave(k_pe), cos[None, :, :], sin[None, :, :])
        q_full = jnp.concatenate([q_nope, q_pe], axis=-1)
        k_full = jnp.concatenate([k_nope, jnp.broadcast_to(k_pe[:, :, None, :], (B, S, H, ROPE))], axis=-1)
        scores = jnp.einsum('bqhd,bkhd->bhqk', q_full, k_full) * softmax_scale
        causal = jnp.tril(jnp.ones((S, S), dtype=bool))
        scores = jnp.where(causal[None, None], scores, jnp.finfo(scores.dtype).min)
        attn = jax.nn.softmax(scores, axis=-1)
        out = jnp.einsum('bhqk,bkhd->bqhd', attn, v).reshape(B, S, H * VD)
        return out @ wo.T

    def _L0_ffn_ref(hidden_states, w_gate, w_up, w_down):
        import jax, jax.numpy as jnp
        import numpy as np
        EPS = 1e-05

        def _bitlinear(x, w):
            scale = jnp.mean(jnp.abs(w))
            q = jnp.round(jnp.clip(w / (scale + EPS), -1.0, 1.0))
            deq = q * scale
            return x @ deq.T
        gate = _bitlinear(hidden_states, w_gate)
        up = _bitlinear(hidden_states, w_up)
        inter = gate * up
        out = _bitlinear(inter, w_down)
        return out
    x = L0_attn_x
    mod = (_silu(L0_c) @ L0_wmod).reshape(L0_c.shape[0], 6, 1, -1)
    sa, ca, ga, sb, cb, gb = (mod[:, 0], mod[:, 1], mod[:, 2], mod[:, 3], mod[:, 4], mod[:, 5])
    ga = (2 * (ga >= 0) - 1) * jnp.maximum(jnp.abs(ga), 0.25)
    gb = (2 * (gb >= 0) - 1) * jnp.maximum(jnp.abs(gb), 0.25)
    h = _layernorm(x, axis=-1) * (1 + ca) + sa
    x = x + ga * _L0_attn_ref(h, L0_attn_wq_a, L0_attn_q_a_ln_w, L0_attn_wq_b, L0_attn_wkv_a, L0_attn_kv_a_ln_w, L0_attn_wkv_b, L0_attn_wo)
    h = _layernorm(x, axis=-1) * (1 + cb) + sb
    x = x + gb * _L0_ffn_ref(h, L0_ffn_w_gate, L0_ffn_w_up, L0_ffn_w_down)
    return x

_drawn_inputs = setup_inputs


def setup_inputs(seed=0):
    import zlib

    import numpy as np

    out = dict(_drawn_inputs(seed))
    spreads = {'L0_attn_q_a_ln_w': (1.0, 0.6), 'L0_attn_kv_a_ln_w': (1.0, 0.6)}
    factors = {'L0_attn_wq_a': 8.0,
     'L0_attn_wq_b': 8.0,
     'L0_attn_wkv_a': 8.0,
     'L0_attn_wkv_b': 8.0,
     'L0_attn_wo': 8.0,
     'L0_ffn_w_gate': 4.886,
     'L0_ffn_w_up': 4.686,
     'L0_ffn_w_down': 4.689,
     'L0_c': 4.392,
     'L0_wmod': 4.354}
    for name, (base, spread) in spreads.items():
        noise = np.random.default_rng([zlib.crc32(name.encode()), seed]).standard_normal(out[name].shape)
        drawn = base * np.exp(spread * noise) if base else spread * noise
        out[name] = jnp.asarray(drawn.astype(out[name].dtype))
    for name, factor in factors.items():
        out[name] = (out[name] * factor).astype(out[name].dtype)
    return out
```

```python
from contextlib import ExitStack

import concourse.bass as bass
from concourse import mybir

F32 = mybir.dt.float32
F32R = mybir.dt.float32r
I32 = mybir.dt.int32
ALU = mybir.AluOpType
ACT = mybir.ActivationFunctionType
AX = mybir.AxisListType

P = 128
B, S, D = 4, 512, 512
H, NOPE, ROPE, VD, KVR, QR = 32, 64, 64, 128, 32, 128
HALF = ROPE // 2
I = 1376
TC = S // P
KC = D // P
IC = (I + P - 1) // P
HG = 4
G = H // HG
QD = KVR + ROPE
QW = HG * QD
QA = QR + KVR + ROPE
TRI = P * TC * (TC + 1) // 2
ONE = 1
NEG = -3.0e38
EPS_LN, EPS_RMS, EPS_BIT = 1e-5, 1e-6, 1e-5
MSCALE = 0.1 * 4.852030263919617 + 1.0
SCALE = (NOPE + ROPE) ** -0.5 * MSCALE * MSCALE

SC_ORDER = [3, 2, 0, 1]
SC_BANK = {3: (0, 0), 2: (1, 0), 0: (1, 384), 1: (0, 0)}
P_OFF = {3: 0, 2: 512, 0: 896, 1: 1024}
T_OFF = {0: 0, 1: 512, 3: 896, 2: 1024}
ACT_COLS = 1024


def rows_of(ic):
    return min(P, I - ic * P)


def adaln_block(nc, x, wa, wqn, wkn, wqp, wv, wo, wg, wu, wd, qln, kvln, cT, wmod, cos, sin2, out, mod_dram):
    top = [(nc.sbuf_base + 31) // 32 * 32]

    def place(name, shape, dt=F32, at=None):
        size = 4
        for n in shape[1:]:
            size *= n
        off = top[0] if at is None else at
        t = nc.alloc_sbuf_tensor_at(name, list(shape), dt, offset=off)
        end = (off + size + 31) // 32 * 32
        if at is None:
            top[0] = end
        return t, end

    ident, _ = place("ident", (P, P))
    ones, _ = place("ones", (P, P))
    mask, _ = place("mask", (P, S))
    cos_sb, _ = place("cos_sb", (P, TC, HALF))
    sin_sb, _ = place("sin_sb", (P, TC, 2, HALF))
    g_sb, _ = place("g_sb", (P, G, D))
    wq_sb, _ = place("wq_sb", (P, G * QW))
    wa_sb, _ = place("wa_sb", (P, KC, QA))
    kvln_sb, _ = place("kvln_sb", (P, KVR))
    qln_sb, _ = place("qln_sb", (P, 1))
    gate_w, _ = place("gate_w", (P, KC, I), F32R)
    up_w, _ = place("up_w", (P, KC, I), F32R)
    down_w, _ = place("down_w", (P, IC, D), F32R)
    bit, _ = place("bit", (P, 12))
    x_sb, _ = place("x_sb", (P, TC, D))
    ut_sb, _ = place("ut_sb", (P, TC, 2 * D))
    gb_sb, _ = place("gb_sb", (P, 2, D))
    modc, _ = place("modc", (P, 4, KC))
    qnT, _ = place("qnT", (P, S))
    kt_sb, _ = place("kt_sb", (P, TC, QD))
    k_hi, _ = place("k_hi", (P, S), F32R)
    k_lo, _ = place("k_lo", (P, S), F32R)
    small, _ = place("small", (P, 128))
    shared = top[0]
    qs, e = place("qs", (P, 2, TC, HG, QD), at=shared)
    q_hi, e = place("q_hi", (P, 2, S), F32R, at=e)
    q_lo, e = place("q_lo", (P, 2, S), F32R, at=e)
    pr, e = place("pr", (P, 2, TRI), at=e)
    pts, e = place("pts", (P, HG, TRI), at=e)
    rot, e = place("rot", (P, 2, 2, 2, HG, HALF), at=e)
    rb, e = place("rb", (P, 2, TC, HG, KVR), at=e)
    rsb, e = place("rsb", (P, S), at=e)
    stat, e = place("stat", (P, 64), at=e)
    end_attn = e
    xn_a, e = place("xn_a", (P, TC, D), at=shared)
    hT, e = place("hT", (P, KC, S), at=e)
    qa_sb, e = place("qa_sb", (P, TC, QA), at=e)
    qtok, e = place("qtok", (P, TC, QR), at=e)
    scr, e = place("scr", (P, TC, QR), at=e)
    krot, e = place("krot", (P, 2, TC, 2, HALF), at=e)
    xn_c, e = place("xn_c", (P, TC, D), at=shared)
    h2, e = place("h2", (P, KC, S), at=e)
    h2_hi, e = place("h2_hi", (P, KC, S), F32R, at=e)
    h2_lo, e = place("h2_lo", (P, KC, S), F32R, at=e)
    gcopy, e = place("gcopy", (P, 2, S), at=e)
    inter, e = place("inter", (P, 2, S), at=e)
    i_hi, e = place("i_hi", (P, 2, S), F32R, at=e)
    i_lo, e = place("i_lo", (P, 2, S), F32R, at=e)
    STG = IC * D
    stage, e = place("stage", (P, 3, STG), at=shared)

    wqn_t = stage[0:NOPE, 2, 0:H * QR].rearrange("p (h r) -> p h r", h=H)
    wkn_t = stage[0:NOPE, 2, H * QR:H * QR + H * KVR].rearrange("p (h c) -> p h c", h=H)
    wv_t = stage[:, 1, 4096:4096 + H * KVR].rearrange("p (h c) -> p h c", h=H)
    c_t = small[:, 0:16]
    ce_t = small[:, 16:32]
    cs_t = small[:, 32:48]
    mrow = stage[0:B, 0, 4096:4096 + 1024]

    ctx = ExitStack()
    ps = ctx.enter_context(nc.psum_tensor("ps", [P, 8, 512], F32))

    def sem(name):
        return ctx.enter_context(nc.semaphore(name))

    su_load = [sem(f"su_load{i}") for i in range(3)]
    su_small = sem("su_small")
    su_c = sem("su_c")
    su_qk = sem("su_qk")
    su_wqp = sem("su_wqp")
    su_wv = sem("su_wv")
    su_id = sem("su_id")
    su_exp = sem("su_exp")
    su_silu = sem("su_silu")
    su_abs = sem("su_abs")
    su_modps = sem("su_modps")
    su_modsb = sem("su_modsb")
    su_modst = sem("su_modst")
    su_wqps = sem("su_wqps")
    su_wqsb = sem("su_wqsb")
    su_gps = sem("su_gps")
    su_gsb = sem("su_gsb")
    su_sum = sem("su_sum")
    su_sumps = sem("su_sumps")
    su_bit = sem("su_bit")
    su_free = sem("su_free")

    with nc.Block() as block:
        @block.sync
        def _(sp):
            sp.dma_start(c_t, cT).then_inc(su_c, 16)
            sp.dma_start(wqn_t, wqn).then_inc(su_qk, 16)
            sp.dma_start(wkn_t, wkn).then_inc(su_qk, 16)
            for i in range(3):
                if i >= 2:
                    sp.wait_ge(su_modps, 2 * (i - 1))
                sp.dma_start(stage[:, i % 2, 0:4096].rearrange("p (k n) -> p k n", k=KC),
                             wmod.rearrange("(k p) n -> p k n", p=P)[:, :, i * 1024:(i + 1) * 1024]
                             ).then_inc(su_load[i % 2], 16)
                sp.wait_ge(su_modsb, 2 * (i + 1))
                sp.dma_start(mod_dram[:, i * 1024:(i + 1) * 1024], mrow).then_inc(su_modst, 16)
                sp.wait_ge(su_modst, 16 * (i + 1))
            sp.dma_start(wa_sb[:], wa.rearrange("(k p) n -> p k n", p=P)).then_inc(su_small, 16)
            sp.dma_start(cos_sb[:], cos.rearrange("(t p) j -> p t j", p=P)).then_inc(su_small, 16)
            sp.dma_start(sin_sb[:], sin2.rearrange("(t p) e j -> p t e j", p=P)).then_inc(su_small, 16)
            sp.dma_start(qln_sb[:], qln).then_inc(su_small, 16)
            sp.dma_start(kvln_sb[:], kvln.partition_broadcast(P)).then_inc(su_small, 16)
            wq_v = wq_sb[:].rearrange("p (g a n) -> p g a n", g=G, a=3)
            sp.dma_start(wq_v[:, :, 1:3, :], wqp).then_inc(su_wqp, 16)
            sp.dma_start(wv_t, wv).then_inc(su_wv, 16)
            for i in range(4):
                sp.wait_ge(su_modps, 6)
                if i >= 2:
                    sp.wait_ge(su_gps, 2 * (i - 1))
                sp.dma_start(stage[:, i % 2, 0:4096].rearrange("p (h n) -> p h n", h=8),
                             wo[:, i * 8:(i + 1) * 8, :]).then_inc(su_load[i % 2], 16)
            sp.wait_ge(su_gps, 8)
            sp.wait_ge(su_wqps, 2)
            sp.dma_start(stage[:, 2, 0:KC * I].rearrange("p (k n) -> p k n", k=KC),
                         wg.rearrange("(k p) n -> p k n", p=P)).then_inc(su_load[2], 16)
            sp.dma_start(stage[:, 0, 0:KC * I].rearrange("p (k n) -> p k n", k=KC),
                         wu.rearrange("(k p) n -> p k n", p=P)).then_inc(su_load[0], 16)
            last = (IC - 1) * D
            sp.wait_ge(su_free, 1)
            sp.dma_start(stage[:, 1, 0:last].rearrange("p (k n) -> p k n", k=IC - 1),
                         wd[0:(IC - 1) * P, :].rearrange("(k p) n -> p k n", p=P)).then_inc(su_load[1], 16)
            sp.dma_start(stage[0:rows_of(IC - 1), 1, last:last + D], wd[(IC - 1) * P:, :]).then_inc(su_load[1], 16)
            sp.wait_ge(su_small, 80)
            sp.wait_ge(su_wqp, 16)

        @block.gpsimd
        def _(pool):
            pool.memset(ident[:], 0.0).then_inc(su_id, 1)
            pool.memset(ones[:], 1.0).then_inc(su_id, 1)
            pool.memset(mask[:], 0.0).then_inc(su_id, 1)
            pool.wait_ge(su_id, 3)
            pool.affine_select(out=ident[:], in_=ident[:], compare_op=ALU.not_equal, fill=1.0, base=0,
                               pattern=[[-1, P]], channel_multiplier=1).then_inc(su_id, 1)
            pool.affine_select(out=mask[:], in_=mask[:], compare_op=ALU.is_ge, fill=NEG, base=S - P,
                               pattern=[[-1, S]], channel_multiplier=1).then_inc(su_id, 1)

        @block.scalar
        def _(act):
            act.wait_ge(su_c, 16)
            act.activation(ce_t, c_t, ACT.Exp, scale=-1.0).then_inc(su_exp, 1)
            for i in range(2):
                act.wait_ge(su_wqps, i + 1)
                act.activation(wq_sb[:].rearrange("p (g a n) -> p g a n", g=G, a=3)[:, 4 * i:4 * i + 4, 0, :],
                               ps[:, 2 + i, :].rearrange("p (g n) -> p g n", g=4), ACT.Copy).then_inc(su_wqsb, 1)
            for g in range(G):
                act.wait_ge(su_gps, g + 1)
                act.activation(g_sb[:, g, :], ps[:, 4 + g % 2, :], ACT.Copy).then_inc(su_gsb, 1)

        @block.tensor
        def _(pe):
            pe.wait_ge(su_qk, 32)
            for h in range(H):
                m = pe.matmul(ps[:, 2 + h // 16, (h % 16) * KVR:(h % 16 + 1) * KVR], wqn_t[:, h, :], wkn_t[:, h, :],
                              start=True, stop=True)
                if h % 16 == 15:
                    m.then_inc(su_wqps, 1)
            pe.wait_ge(su_silu, 3)
            for i in range(3):
                pe.wait_ge(su_load[i % 2], 16 * (i // 2 + 1))
                for n in range(2):
                    if 2 * i + n >= 2:
                        pe.wait_ge(su_modsb, 2 * i + n - 1)
                    for k in range(KC):
                        m = pe.matmul(ps[0:B, n, :], cs_t[:, k * B:(k + 1) * B],
                                      stage[:, i % 2, k * 1024 + n * 512:k * 1024 + (n + 1) * 512],
                                      start=(k == 0), stop=(k == KC - 1))
                    m.then_inc(su_modps, 1)
            pe.wait_ge(su_wv, 16)
            for g in range(G):
                i = g // 2
                pe.wait_ge(su_load[i % 2], 16 * ((2 if i % 2 == 0 else 1) + i // 2 + 1))
                if g >= 2:
                    pe.wait_ge(su_gsb, g - 1)
                for j in range(HG):
                    h = g * HG + j
                    m = pe.matmul(ps[j * KVR:(j + 1) * KVR, 4 + g % 2, :], wv_t[:, h, :],
                                  stage[:, i % 2, (h % 8) * D:(h % 8 + 1) * D], start=True, stop=True)
                m.then_inc(su_gps, 1)
            pe.wait_ge(su_sum, 3)
            pe.wait_ge(su_id, 2)
            pe.matmul(ps[:, 6, 0:3], ones[:], bit[:, 0:3], start=True, stop=True).then_inc(su_sumps, 1)

        @block.vector
        def _(dve):
            dve.wait_ge(su_exp, 1)
            dve.tensor_scalar(ce_t, ce_t, 1.0, None, ALU.add).then_inc(su_silu, 1)
            dve.wait_ge(su_silu, 1)
            dve.reciprocal(cs_t, ce_t).then_inc(su_silu, 1)
            dve.wait_ge(su_silu, 2)
            dve.tensor_tensor(cs_t, cs_t, c_t, ALU.mult).then_inc(su_silu, 1)
            for i in range(3):
                if i >= 1:
                    dve.wait_ge(su_modst, 16 * i)
                for n in range(2):
                    dve.wait_ge(su_modps, 2 * i + n + 1)
                    dve.tensor_copy(mrow[:, n * 512:(n + 1) * 512], ps[0:B, n, :]).then_inc(su_modsb, 1)
            dve.wait_ge(su_gps, 8)
            dve.memset(stage[:, 1, (IC - 1) * D:], 0.0).then_inc(su_free, 1)
            order = [(2, 0, gate_w, KC * I, 1), (0, 1, up_w, KC * I, 4), (1, 2, down_w, IC * D, 0)]
            need = [16, 16 * 5, 16 * 5]
            for (slot, n, w, cols, _), v in zip(order, need):
                dve.wait_ge(su_load[slot], v)
                dve.tensor_reduce(bit[:, n:n + 1], stage[:, slot, 0:cols], AX.X, ALU.add,
                                  apply_absolute_value=True).then_inc(su_sum, 1)
            dve.wait_ge(su_sumps, 1)
            dve.tensor_scalar(bit[:, 3:6], ps[:, 6, 0:3], 1.0 / (I * D), None, ALU.mult).then_inc(su_bit, 1)
            dve.wait_ge(su_bit, 1)
            dve.tensor_scalar(bit[:, 0:3], bit[:, 3:6], EPS_BIT, 0.5, ALU.add, ALU.mult).then_inc(su_bit, 1)
            dve.tensor_tensor(bit[:, 6:7], bit[:, 3:4], bit[:, 4:5], ALU.mult).then_inc(su_bit, 1)
            dve.wait_ge(su_bit, 3)
            dve.tensor_tensor(bit[:, 7:8], bit[:, 6:7], bit[:, 5:6], ALU.mult).then_inc(su_bit, 1)
            dve.tensor_scalar(bit[:, 8:11], bit[:, 0:3], -1.0, None, ALU.mult).then_inc(su_bit, 1)
            dve.wait_ge(su_bit, 5)
            for k, (slot, n, w, cols, _) in enumerate(order):
                wf = w[:].rearrange("p a b -> p (a b)")
                raw = stage[:, slot, 0:cols]
                dve.tensor_scalar(wf, raw, bit[:, 8 + n:9 + n], None, ALU.is_lt).then_inc(su_bit, 1)
                dve.wait_ge(su_bit, 5 + 2 * k + 1)
                dve.scalar_tensor_tensor(wf, raw, bit[:, n:n + 1], wf.bitcast(F32), ALU.is_gt,
                                         ALU.subtract).then_inc(su_bit, 1)
            dve.wait_ge(su_bit, 5 + 6)

    waits_passed = sem("waits_passed")
    x_in = sem("x_in")
    modc_in = sem("modc_in")
    gb_in = sem("gb_in")
    x2_done = sem("x2_done")
    gb_used = sem("gb_used")
    y_done = sem("y_done")
    y_out = sem("y_out")
    chain = sem("chain")
    xn_done = sem("xn_done")
    tr_done = sem("tr_done")
    hT_done = sem("hT_done")
    qa_ps = sem("qa_ps")
    qa_done = sem("qa_done")
    tok_done = sem("tok_done")
    lat_tr = sem("lat_tr")
    qnT_done = sem("qnT_done")
    kh_done = sem("kh_done")
    kl_done = sem("kl_done")
    qg_done = sem("qg_done")
    qg_abs = sem("qg_abs")
    qg_rot = sem("qg_rot")
    qs_done = sem("qs_done")
    q_tr = sem("q_tr")
    qh_done = sem("qh_done")
    ql_done = sem("ql_done")
    s_done = sem("s_done")
    s_red = sem("s_red")
    negm = sem("negm")
    p_done = sem("p_done")
    pt_done = sem("pt_done")
    pts_act = sem("pts_act")
    pts_dve = sem("pts_dve")
    rs_done = sem("rs_done")
    rb_done = sem("rb_done")
    av_done = sem("av_done")
    r_done = sem("r_done")
    rsb_done = sem("rsb_done")
    ut_done = sem("ut_done")
    op_done = sem("op_done")
    h2hi_done = sem("h2hi_done")
    h2lo_done = sem("h2lo_done")
    gate_ps = sem("gate_ps")
    up_ps = sem("up_ps")
    gc_done = sem("gc_done")
    in_done = sem("in_done")
    ihi_done = sem("ihi_done")
    ilo_done = sem("ilo_done")
    dn_used = sem("dn_used")
    dn_done = sem("dn_done")

    x_v = x.rearrange("b (t p) d -> b p t d", p=P)
    out_v = out.rearrange("b (t p) d -> b p t d", p=P)
    mod_c = mod_dram.rearrange("b (m k p) -> b p m k", m=6, p=P)
    mod_r = mod_dram.rearrange("b (m n) -> b m n", m=6)
    N_CHAIN = 93

    def steps(eng, b, step):
        with eng.Fori(0, H // 8 - 1) as it:
            for j in range(8):
                step(b * H + it * 8, b * G + it * 2, it * 2, j, False)
        it = H // 8 - 1
        for j in range(8):
            step(b * H + it * 8, b * G + it * 2, it * 2, j, True)

    from_one = [x2_done, y_done, s_done, av_done, pts_act, pts_dve, rsb_done, qg_abs, qg_rot, qh_done, ql_done,
                s_red, ut_done, q_tr]

    def alone(eng):
        eng.sem_inc(waits_passed, 1)

    with nc.Block() as block:
        @block.sync
        def _(sp):
            for s_ in from_one:
                sp.sem_inc(s_, ONE)
            with sp.Fori(0, B) as b:
                sp.wait_ge(x2_done, ONE + b * TC)
                alone(sp)
                sp.dma_start(x_sb[:], x_v[b]).then_inc(x_in, 16)
                sp.wait_ge(y_done, ONE + b * TC)
                alone(sp)
                for m, a in enumerate((0, 1, 3, 4)):
                    sp.dma_start(modc[:, m, :], mod_c[b, :, a, :], allow_slow_non_contiguous=True).then_inc(modc_in, 16)
                for m, a in enumerate((2, 5)):
                    sp.dma_start(gb_sb[:, m, :], mod_r[b, a, :].partition_broadcast(P)).then_inc(gb_in, 16)
                for t in range(TC):
                    sp.wait_ge(y_done, ONE + b * TC + t + 1)
                    alone(sp)
                    sp.dma_start(out_v[b, :, t, :], ut_sb[:, t, 0:D]).then_inc(y_out, 16)
                sp.wait_ge(y_out, (b + 1) * (16 * TC))
                alone(sp)

        @block.gpsimd
        def _(pool):
            def rotate(pb, p, G_par, tc, first):
                pool.wait_ge(qg_rot, ONE + (pb + p + 1) * 2)
                if not first:
                    pool.wait_ge(q_tr, ONE + pb + 4 * (p // 4 - 1))
                r = rot[:, p % 2]
                o = qs[:, G_par, tc]
                pool.tensor_tensor(o[:, :, KVR:KVR + HALF], r[:, 0, 0], r[:, 1, 1], ALU.add).then_inc(qs_done, 1)
                pool.tensor_tensor(o[:, :, KVR + HALF:QD], r[:, 0, 1], r[:, 1, 0], ALU.add).then_inc(qs_done, 1)

            with pool.Fori(0, B) as b:
                for p in range(7):
                    rotate(b * H, p, p // 4, p % 4, p < 4)

                def step(ub, gb, gl, j, last):
                    pool.wait_ge(rs_done, ub + j + 1)
                    alone(pool)
                    pool.tensor_copy(rb[:, j // 4, :, j % 4, :],
                                     stat[:, 32 + 4 * (j % 4):36 + 4 * (j % 4)].unsqueeze(2).broadcast_to((P, TC, KVR))
                                     ).then_inc(rb_done, 1)
                    p = j + 7
                    if not (last and p >= 8):
                        rotate(ub, p, (p // 4) % 2, p % 4, False)
                steps(pool, b, step)

        @block.scalar
        def _(act):
            def q_abs(ub, p, first):
                act.wait_ge(qg_rot, ONE + (ub + p + 1) * 2)
                if not first:
                    act.wait_ge(q_tr, ONE + ub + 4 * (p // 4 - 1))
                act.activation(qs[:, (p // 4) % 2, p % 4, :, 0:KVR],
                               ps[:, 7, 0:HG * KVR].rearrange("p (h c) -> p h c", h=HG), ACT.Copy).then_inc(qg_abs, 1)

            def q_high(ub, v):
                act.wait_ge(q_tr, ONE + ub + v + 1)
                if v >= 1:
                    act.wait_ge(s_done, ONE + (ub + v - 1) * 4)
                act.activation(q_hi[0:QD, v % 2, :], ps[0:QD, 5, :], ACT.Copy).then_inc(qh_done, 1)

            def exps(ub, x_):
                act.wait_ge(negm, ub + x_ + 1)
                for i, qc in enumerate(SC_ORDER):
                    n = (qc + 1) * P
                    pp = pr[:, x_ % 2, P_OFF[qc]:P_OFF[qc] + n]
                    m = act.activation(pp, pp, ACT.Exp, bias=stat[:, 8 + 4 * (x_ % 2) + qc:9 + 4 * (x_ % 2) + qc],
                                       scale=SCALE, accum_out=stat[:, 16 + 4 * (x_ % 4) + qc:17 + 4 * (x_ % 4) + qc])
                m.then_inc(p_done, 1)

            with act.Fori(0, B) as b:
                act.wait_ge(chain, b * N_CHAIN + 1)
                for k in range(KC):
                    act.wait_ge(tr_done, b * (2 * KC) + k + 1)
                    act.activation(hT[:, k, :], ps[:, k, :], ACT.Identity, bias=modc[:, 0, k:k + 1],
                                   scale=modc[:, 1, k:k + 1]).then_inc(hT_done, 1)
                act.wait_ge(qa_ps, b + 1)
                act.activation(qa_sb[:].rearrange("p (a t) n -> p a t n", a=2),
                               ps[:, 4:6, :].rearrange("p a (t n) -> p a t n", t=2)[:, :, :, 0:QA],
                               ACT.Copy).then_inc(qa_done, 1)
                act.wait_ge(lat_tr, b * 2 + 1)
                act.activation(qnT[:], ps[:, 6, :], ACT.Copy, scale=qln_sb[:, 0:1]).then_inc(qnT_done, 1)
                act.wait_ge(lat_tr, b * 2 + 2)
                act.activation(k_hi[0:QD, :], ps[0:QD, 7, :], ACT.Copy).then_inc(kh_done, 1)
                for p in range(4):
                    q_abs(b * H, p, True)
                q_high(b * H, 0)
                for p in range(4, 7):
                    q_abs(b * H, p, False)
                q_high(b * H, 1)
                exps(b * H, 0)
                q_high(b * H, 2)

                def step(ub, gb, gl, j, last):
                    g = j // 4
                    if not (last and j + 1 >= 8):
                        exps(ub, j + 1)
                    act.wait_ge(pt_done, ub + j + 1)
                    act.wait_ge(av_done, ONE + gb + g)
                    act.activation(pts[:, j % 4, 0:ACT_COLS],
                                   ps[:, 2:5, :].rearrange("p a n -> p (a n)")[:, 0:ACT_COLS],
                                   ACT.Copy).then_inc(pts_act, 1)
                    if not (last and j + 3 >= 8):
                        q_high(ub, j + 3)
                    if j % 4 == 3:
                        act.wait_ge(r_done, gb + g + 1)
                        act.activation(rsb[:], ps[:, 6, :], ACT.Copy).then_inc(rsb_done, 1)
                    if not (last and j + 7 >= 8):
                        q_abs(ub, j + 7, False)
                steps(act, b, step)

                for k in range(KC):
                    act.wait_ge(tr_done, b * (2 * KC) + KC + k + 1)
                    act.activation(h2[:, k, :], ps[:, 4 + k, :], ACT.Identity, bias=modc[:, 2, k:k + 1],
                                   scale=modc[:, 3, k:k + 1]).then_inc(hT_done, 1)
                    act.wait_ge(hT_done, b * (2 * KC) + KC + k + 1)
                    act.activation(h2_hi[:, k, :], h2[:, k, :], ACT.Copy).then_inc(h2hi_done, 1)
                for ic in range(IC):
                    M = rows_of(ic)
                    act.wait_ge(gate_ps, b * IC + ic + 1)
                    if ic >= 2:
                        act.wait_ge(in_done, b * IC + ic - 1)
                    act.activation(gcopy[0:M, ic % 2, :], ps[0:M, 4 + 2 * (ic % 2), :], ACT.Copy).then_inc(gc_done, 1)
                    act.wait_ge(in_done, b * IC + ic + 1)
                    if ic >= 2:
                        act.wait_ge(dn_used, b * (IC - 1) + ic - 1)
                    act.activation(i_hi[0:M, ic % 2, :], inter[0:M, ic % 2, :], ACT.Copy).then_inc(ihi_done, 1)

        @block.tensor
        def _(pe):
            def q_gen(ub, p, gl, gb):
                pe.wait_ge(qg_abs, ONE + ub + p)
                pe.wait_ge(qg_rot, ONE + (ub + p) * 2)
                tc = p % 4
                g0 = gl + p // 4
                w = wq_sb[:, bass.ds(g0 * QW, QW)]
                pe.matmul(ps[:, 7, 0:QW], qnT[:, tc * P:(tc + 1) * P], w, start=True, stop=True).then_inc(qg_done, 1)

            def q_transpose(ub, v):
                pe.wait_ge(qs_done, (ub + 4 * (v // 4) + 4) * 2)
                pe.wait_ge(qg_abs, ONE + ub + 4 * (v // 4) + 4)
                pe.wait_ge(qh_done, ONE + ub + v)
                pe.wait_ge(ql_done, ONE + ub + v)
                for tc in range(TC):
                    m = pe.transpose(ps[0:QD, 5, tc * P:(tc + 1) * P], qs[:, (v // 4) % 2, tc, v % 4, :], ident[:])
                m.then_inc(q_tr, 1)

            def scores(ub, w):
                pe.wait_ge(qh_done, ONE + ub + w + 1)
                pe.wait_ge(ql_done, ONE + ub + w + 1)
                pe.wait_ge(s_red, ONE + (ub + w) * 4)
                for i, qc in enumerate(SC_ORDER):
                    if i == 3:
                        pe.wait_ge(s_red, ONE + (ub + w) * 4 + 1)
                    bank, off = SC_BANK[qc]
                    n = (qc + 1) * P
                    o = ps[:, bank, off:off + n]
                    q = slice(qc * P, (qc + 1) * P)
                    pe.matmul(o, q_hi[0:QD, w % 2, q], k_hi[0:QD, 0:n], start=True, stop=False)
                    pe.matmul(o, q_hi[0:QD, w % 2, q], k_lo[0:QD, 0:n], start=False, stop=False)
                    pe.matmul(o, q_lo[0:QD, w % 2, q], k_hi[0:QD, 0:n], start=False, stop=True).then_inc(s_done, 1)

            with pe.Fori(0, B) as b:
                pe.wait_ge(xn_done, b * (2 * TC) + TC)
                for k in range(KC):
                    for t in range(TC):
                        m = pe.transpose(ps[:, k, t * P:(t + 1) * P], xn_a[:, t, k * P:(k + 1) * P], ident[:])
                    m.then_inc(tr_done, 1)
                pe.wait_ge(hT_done, b * (2 * KC) + KC)
                for t in range(TC):
                    for k in range(KC):
                        m = pe.matmul(ps[:, 4 + t // 2, (t % 2) * 256:(t % 2) * 256 + QA], hT[:, k, t * P:(t + 1) * P],
                                      wa_sb[:, k, :], start=(k == 0), stop=(k == KC - 1))
                m.then_inc(qa_ps, 1)
                pe.wait_ge(tok_done, (b + 1) * 2)
                for t in range(TC):
                    m = pe.transpose(ps[:, 6, t * P:(t + 1) * P], qtok[:, t, :], ident[:])
                m.then_inc(lat_tr, 1)
                for t in range(TC):
                    m = pe.transpose(ps[0:QD, 7, t * P:(t + 1) * P], kt_sb[:, t, :], ident[:])
                m.then_inc(lat_tr, 1)
                pe.wait_ge(qnT_done, b + 1)
                pe.wait_ge(kh_done, b + 1)
                pe.wait_ge(kl_done, b + 1)
                for p in range(4):
                    q_gen(b * H, p, 0, b * G)
                q_transpose(b * H, 0)
                scores(b * H, 0)
                for p in range(4, 7):
                    q_gen(b * H, p, 0, b * G)
                q_transpose(b * H, 1)
                scores(b * H, 1)
                q_transpose(b * H, 2)

                def step(ub, gb, gl, j, last):
                    g = j // 4
                    pe.wait_ge(p_done, ub + j + 1)
                    pe.wait_ge(pts_act, ONE + ub + j)
                    pe.wait_ge(pts_dve, ONE + ub + j)
                    for kc in range(TC):
                        for qc in range(kc, TC):
                            off = T_OFF[kc] + (qc - kc) * P
                            m = pe.transpose(ps[:, 2 + off // 512, off % 512:off % 512 + P],
                                             pr[:, j % 2, P_OFF[qc] + kc * P:P_OFF[qc] + (kc + 1) * P], ident[:])
                    m.then_inc(pt_done, 1)
                    if not (last and j + 7 >= 8):
                        q_gen(ub, j + 7, gl, gb + g)
                    if not (last and j + 3 >= 8):
                        q_transpose(ub, j + 3)
                    if j % 4 == 3:
                        pe.wait_ge(rb_done, ub + j + 1)
                        pe.wait_ge(ut_done, ONE + gb + g)
                        for qc in range(TC):
                            m = pe.transpose(ps[:, 6, qc * P:(qc + 1) * P],
                                             rb[:, g, qc].rearrange("p h c -> p (h c)"), ident[:])
                        m.then_inc(r_done, 1)
                    if not (last and j + 2 >= 8):
                        scores(ub, j + 2)
                    if j % 4 == 3:
                        pe.wait_ge(pts_act, ONE + ub + j + 1)
                        pe.wait_ge(pts_dve, ONE + ub + j + 1)
                        pe.wait_ge(rsb_done, ONE + gb + g + 1)
                        for kc in range(TC):
                            for h in range(HG):
                                m = pe.matmul(ps[h * KVR:(h + 1) * KVR, 6, kc * P:], kt_sb[:, kc, 0:KVR],
                                              pts[:, h, T_OFF[kc]:T_OFF[kc] + S - kc * P],
                                              start=(kc == 0), stop=(kc == TC - 1))
                        m.then_inc(av_done, 1)
                steps(pe, b, step)

                pe.wait_ge(ut_done, ONE + (b + 1) * G)
                for t in range(TC):
                    for g in range(G):
                        m = pe.matmul(ps[:, t, :], ut_sb[:, t, g * P:(g + 1) * P], g_sb[:, g, :],
                                      start=(g == 0), stop=(g == G - 1))
                    m.then_inc(op_done, 1)
                pe.wait_ge(xn_done, (b + 1) * (2 * TC))
                for k in range(KC):
                    for t in range(TC):
                        m = pe.transpose(ps[:, 4 + k, t * P:(t + 1) * P], xn_c[:, t, k * P:(k + 1) * P], ident[:])
                    m.then_inc(tr_done, 1)
                pe.wait_ge(h2hi_done, (b + 1) * KC)
                pe.wait_ge(h2lo_done, (b + 1) * KC)

                def down(ic):
                    M = rows_of(ic)
                    pe.wait_ge(ihi_done, b * IC + ic + 1)
                    pe.wait_ge(ilo_done, b * IC + ic + 1)
                    for t in range(TC):
                        for n, w in enumerate((i_hi, i_lo)):
                            m = pe.matmul(ps[:, t, :], w[0:M, ic % 2, t * P:(t + 1) * P], down_w[0:M, ic, :],
                                          start=(ic == 0 and n == 0), stop=(ic == IC - 1 and n == 1))
                        if ic == IC - 1:
                            m.then_inc(dn_done, 1)
                    if ic < IC - 1:
                        m.then_inc(dn_used, 1)

                for ic in range(IC):
                    M = rows_of(ic)
                    if ic >= 2:
                        pe.wait_ge(in_done, b * IC + ic - 1)
                    for w, bank, s_ in ((gate_w, 4, gate_ps), (up_w, 5, up_ps)):
                        for k in range(KC):
                            for n, a in enumerate((h2_hi, h2_lo)):
                                m = pe.matmul(ps[0:M, bank + 2 * (ic % 2), :], w[:, k, ic * P:ic * P + M], a[:, k, :],
                                              start=(k == 0 and n == 0), stop=(k == KC - 1 and n == 1))
                        m.then_inc(s_, 1)
                    if ic >= 1:
                        down(ic - 1)
                down(IC - 1)

        @block.vector
        def _(dve):
            def q_rot(ub, p):
                dve.wait_ge(qg_done, ub + p + 1)
                if p >= 2:
                    dve.wait_ge(qs_done, (ub + p - 1) * 2)
                xq = ps[:, 7, HG * KVR:QW].rearrange("p (e h j) -> p e h j", e=2, h=HG)
                tc = p % 4
                dve.tensor_tensor(rot[:, p % 2, 0], xq,
                                  cos_sb[:, tc, :].unsqueeze(1).unsqueeze(1).broadcast_to((P, 2, HG, HALF)),
                                  ALU.mult).then_inc(qg_rot, 1)
                dve.tensor_tensor(rot[:, p % 2, 1], xq,
                                  sin_sb[:, tc].unsqueeze(2).broadcast_to((P, 2, HG, HALF)),
                                  ALU.mult).then_inc(qg_rot, 1)

            def q_low(ub, v):
                dve.wait_ge(qh_done, ONE + ub + v + 1)
                dve.tensor_tensor(q_lo[0:QD, v % 2, :], ps[0:QD, 5, :], q_hi[0:QD, v % 2, :].bitcast(F32),
                                  ALU.subtract).then_inc(ql_done, 1)

            def maxes(ub, w):
                if w >= 2:
                    dve.wait_ge(pt_done, ub + w - 1)
                for i, qc in enumerate(SC_ORDER):
                    if i != 2:
                        dve.wait_ge(s_done, ONE + (ub + w) * 4 + (1, 3, 3, 4)[i])
                        alone(dve)
                    bank, off = SC_BANK[qc]
                    n = (qc + 1) * P
                    dve.tensor_tensor_reduce(pr[:, w % 2, P_OFF[qc]:P_OFF[qc] + n], ps[:, bank, off:off + n],
                                             mask[:, S - n:S], 1.0, NEG, ALU.add, ALU.max,
                                             stat[:, 4 * (w % 2) + qc:4 * (w % 2) + qc + 1]).then_inc(s_red, 1)
                dve.wait_ge(s_red, ONE + (ub + w + 1) * 4)
                if w >= 2:
                    dve.wait_ge(p_done, ub + w - 1)
                dve.tensor_scalar(stat[:, 8 + 4 * (w % 2):12 + 4 * (w % 2)], stat[:, 4 * (w % 2):4 + 4 * (w % 2)],
                                  -SCALE, None, ALU.mult).then_inc(negm, 1)

            with dve.Fori(0, B) as b:
                n_chain = [0]

                def link(ins):
                    n_chain[0] += 1
                    ins.then_inc(chain, 1)

                def linked():
                    dve.wait_ge(chain, b * N_CHAIN + n_chain[0])

                def rsqrt(y, v, eps, n):
                    a, t = small[:, 64:64 + n], small[:, 72:72 + n]
                    link(dve.tensor_scalar(a, v, eps, None, ALU.add))
                    linked()
                    link(dve.tensor_scalar(t.bitcast(I32), a.bitcast(I32), 1, None, ALU.logical_shift_right))
                    linked()
                    link(dve.tensor_scalar(y.bitcast(I32), t.bitcast(I32), -1.0, float(0x5f3759df), ALU.mult, ALU.add))
                    linked()
                    for _ in range(4):
                        link(dve.tensor_tensor(t, y, y, ALU.mult))
                        linked()
                        link(dve.scalar_tensor_tensor(t, t, -0.5, a, ALU.mult, ALU.mult))
                        linked()
                        link(dve.scalar_tensor_tensor(y, t, 1.5, y, ALU.add, ALU.mult))
                        linked()

                def layernorm(src, dst):
                    for t in range(TC):
                        link(dve.bn_stats(small[:, 6 * t:6 * t + 6], src(t)))
                    linked()
                    alone(dve)
                    for t in range(TC):
                        link(dve.bn_aggr(small[:, 24 + 2 * t:26 + 2 * t], small[:, 6 * t:6 * t + 6]))
                    linked()
                    mv = small[:, 24:32].rearrange("p (t e) -> p t e", e=2)
                    rsqrt(small[:, 32:36], mv[:, :, 1], EPS_LN, 4)
                    for t in range(TC):
                        dve.tensor_scalar(dst[:, t, :], src(t), small[:, 24 + 2 * t:25 + 2 * t],
                                          small[:, 32 + t:33 + t], ALU.subtract, ALU.mult).then_inc(xn_done, 1)

                dve.wait_ge(modc_in, (b + 1) * 64)
                sc_rows = modc[:].rearrange("p (e f) k -> p e f k", f=2)[:, :, 1, :]
                link(dve.tensor_scalar(sc_rows, sc_rows, 1.0, None, ALU.add))
                dve.wait_ge(gb_in, (b + 1) * 32)
                size = ut_sb[:, 0:2, 0:D]
                link(dve.scalar_tensor_tensor(size, gb_sb[:], -1.0, gb_sb[:], ALU.mult, ALU.max))
                linked()
                link(dve.tensor_scalar(gb_sb[:], gb_sb[:], 0.0, 2.0, ALU.is_ge, ALU.mult))
                linked()
                link(dve.tensor_scalar(gb_sb[:], gb_sb[:], -1.0, None, ALU.add))
                linked()
                link(dve.scalar_tensor_tensor(gb_sb[:], size, 0.25, gb_sb[:], ALU.max, ALU.mult))
                linked()
                link(dve.tensor_scalar(gb_sb[:, 1, :], gb_sb[:, 1, :], bit[:, 7:8], None, ALU.mult))
                linked()

                dve.wait_ge(x_in, (b + 1) * 16)
                layernorm(lambda t: x_sb[:, t, :], xn_a)
                dve.wait_ge(qa_done, b + 1)
                for t in range(TC):
                    link(dve.tensor_tensor_reduce(scr[:, t, :], qa_sb[:, t, 0:QR], qa_sb[:, t, 0:QR], 1.0 / QR, 0.0,
                                                  ALU.mult, ALU.add, small[:, 40 + t:41 + t]))
                    link(dve.tensor_tensor_reduce(krot[:, 0, t, 0, :], qa_sb[:, t, QR:QR + KVR],
                                                  qa_sb[:, t, QR:QR + KVR], 1.0 / KVR, 0.0,
                                                  ALU.mult, ALU.add, small[:, 44 + t:45 + t]))
                linked()
                rsqrt(small[:, 48:56], small[:, 40:48], EPS_RMS, 8)
                for t in range(TC):
                    link(dve.tensor_scalar(qtok[:, t, :], qa_sb[:, t, 0:QR], small[:, 48 + t:49 + t], None, ALU.mult))
                    link(dve.scalar_tensor_tensor(kt_sb[:, t, 0:KVR], qa_sb[:, t, QR:QR + KVR],
                                                  small[:, 52 + t:53 + t], kvln_sb[:], ALU.mult, ALU.mult))
                xk = qa_sb[:, :, QR + KVR:QA].rearrange("p t (e j) -> p t e j", e=2)
                link(dve.tensor_tensor(krot[:, 0], xk, cos_sb[:].unsqueeze(2).broadcast_to((P, TC, 2, HALF)), ALU.mult))
                link(dve.tensor_tensor(krot[:, 1], xk, sin_sb[:], ALU.mult))
                linked()
                dve.tensor_tensor(kt_sb[:, :, KVR:KVR + HALF], krot[:, 0, :, 0], krot[:, 1, :, 1],
                                  ALU.add).then_inc(tok_done, 1)
                dve.tensor_tensor(kt_sb[:, :, KVR + HALF:QD], krot[:, 0, :, 1], krot[:, 1, :, 0],
                                  ALU.add).then_inc(tok_done, 1)
                dve.wait_ge(kh_done, b + 1)
                dve.tensor_tensor(k_lo[0:QD, :], ps[0:QD, 7, :], k_hi[0:QD, :].bitcast(F32),
                                  ALU.subtract).then_inc(kl_done, 1)
                for p in range(4):
                    q_rot(b * H, p)
                q_low(b * H, 0)
                maxes(b * H, 0)
                for p in range(4, 7):
                    q_rot(b * H, p)
                q_low(b * H, 1)
                maxes(b * H, 1)
                q_low(b * H, 2)

                def step(ub, gb, gl, j, last):
                    g = j // 4
                    dve.wait_ge(pt_done, ub + j + 1)
                    dve.wait_ge(av_done, ONE + gb + g)
                    dve.tensor_copy(pts[:, j % 4, ACT_COLS:TRI], ps[:, 4, 0:TRI - ACT_COLS]).then_inc(pts_dve, 1)
                    dve.reciprocal(stat[:, 32 + 4 * (j % 4):36 + 4 * (j % 4)],
                                   stat[:, 16 + 4 * (j % 4):20 + 4 * (j % 4)]).then_inc(rs_done, 1)
                    if not (last and j + 7 >= 8):
                        q_rot(ub, j + 7)
                    if not (last and j + 2 >= 8):
                        maxes(ub, j + 2)
                    if not (last and j + 3 >= 8):
                        q_low(ub, j + 3)
                    if j % 4 == 3:
                        dve.wait_ge(av_done, ONE + gb + g + 1)
                        dve.wait_ge(rsb_done, ONE + gb + g + 1)
                        dve.tensor_tensor(ut_sb[:, :, bass.ds((gl + g) * P, P)],
                                          ps[:, 6, :].rearrange("p (t n) -> p t n", t=TC),
                                          rsb[:].rearrange("p (t n) -> p t n", t=TC), ALU.mult).then_inc(ut_done, 1)
                steps(dve, b, step)

                for t in range(TC):
                    dve.wait_ge(op_done, b * TC + t + 1)
                    link(dve.tensor_tensor(ut_sb[:, t, 0:D], ps[:, t, :], gb_sb[:, 0, :], ALU.mult))
                    linked()
                    dve.tensor_tensor(ut_sb[:, t, 0:D], ut_sb[:, t, 0:D], x_sb[:, t, :], ALU.add).then_inc(x2_done, 1)
                dve.wait_ge(x2_done, ONE + (b + 1) * TC)
                layernorm(lambda t: ut_sb[:, t, 0:D], xn_c)
                for k in range(KC):
                    dve.wait_ge(h2hi_done, b * KC + k + 1)
                    dve.tensor_tensor(h2_lo[:, k, :], h2[:, k, :], h2_hi[:, k, :].bitcast(F32),
                                      ALU.subtract).then_inc(h2lo_done, 1)
                for ic in range(IC):
                    M = rows_of(ic)
                    dve.wait_ge(gc_done, b * IC + ic + 1)
                    dve.wait_ge(up_ps, b * IC + ic + 1)
                    if ic >= 2:
                        dve.wait_ge(ihi_done, b * IC + ic - 1)
                        dve.wait_ge(ilo_done, b * IC + ic - 1)
                    dve.tensor_tensor(inter[0:M, ic % 2, :], ps[0:M, 5 + 2 * (ic % 2), :], gcopy[0:M, ic % 2, :],
                                      ALU.mult).then_inc(in_done, 1)
                    dve.wait_ge(ihi_done, b * IC + ic + 1)
                    if ic >= 2:
                        dve.wait_ge(dn_used, b * (IC - 1) + ic - 1)
                    dve.tensor_tensor(i_lo[0:M, ic % 2, :], inter[0:M, ic % 2, :], i_hi[0:M, ic % 2, :].bitcast(F32),
                                      ALU.subtract).then_inc(ilo_done, 1)
                for t in range(TC):
                    dve.wait_ge(dn_done, b * TC + t + 1)
                    link(dve.tensor_tensor(xn_c[:, t, :], ps[:, t, :], gb_sb[:, 1, :], ALU.mult))
                    linked()
                    dve.tensor_tensor(ut_sb[:, t, 0:D], xn_c[:, t, :], ut_sb[:, t, 0:D], ALU.add).then_inc(y_done, 1)
                dve.wait_ge(y_out, (b + 1) * (16 * TC))
                assert n_chain[0] == N_CHAIN, n_chain[0]
    ctx.close()


def rope_tables():
    import math
    import numpy as np
    base, factor, orig = 10000.0, 128.0, 1024

    def corr_dim(r):
        return ROPE * math.log(orig / (r * 2 * math.pi)) / (2 * math.log(base))
    low = max(math.floor(corr_dim(32.0)), 0)
    high = min(math.ceil(corr_dim(1.0)), ROPE - 1)
    hi = high + 0.001 if low == high else float(high)
    ramp = np.clip((np.arange(HALF, dtype=np.float32) - low) / (hi - low), 0.0, 1.0)
    inv_freq_mask = 1.0 - ramp
    extra = 1.0 / base ** (np.arange(0, ROPE, 2, dtype=np.float32) / ROPE)
    inv_freq = extra / factor * (1.0 - inv_freq_mask) + extra * inv_freq_mask
    freqs = np.outer(np.arange(S, dtype=np.float32), inv_freq)
    cos, sin = np.cos(freqs).astype(np.float32), np.sin(freqs).astype(np.float32)
    return cos, np.ascontiguousarray(np.stack([sin, -sin], 1))


def kernel(L0_attn_x, L0_attn_wq_a, L0_attn_q_a_ln_w, L0_attn_wq_b, L0_attn_wkv_a, L0_attn_kv_a_ln_w, L0_attn_wkv_b,
           L0_attn_wo, L0_ffn_w_gate, L0_ffn_w_up, L0_ffn_w_down, L0_c, L0_wmod):
    import numpy as np
    import concourse.bacc as bacc
    from concourse.bass_utils import run_bass_kernel_spmd

    con = np.ascontiguousarray
    wq = np.asarray(L0_attn_wq_b).reshape(H, NOPE + ROPE, QR)
    wkv = np.asarray(L0_attn_wkv_b).reshape(H, NOPE + VD, KVR)
    kv_a = np.asarray(L0_attn_wkv_a)
    wa = con(np.concatenate([np.asarray(L0_attn_wq_a), kv_a[:KVR], kv_a[KVR::2], kv_a[KVR + 1::2]], 0).T)
    pe = wq[:, NOPE:].reshape(G, HG, HALF, 2, QR)
    cos, sin2 = rope_tables()
    arrays = {
        "x": con(L0_attn_x),
        "wa": wa,
        "wqn": con(wq[:, :NOPE].transpose(1, 0, 2)),
        "wkn": con(wkv[:, :NOPE].transpose(1, 0, 2)),
        "wqp": con(pe.transpose(4, 0, 3, 1, 2).reshape(QR, G, 2, HG * HALF)),
        "wv": con(wkv[:, NOPE:].transpose(1, 0, 2)),
        "wo": con(np.asarray(L0_attn_wo).reshape(D, H, VD).transpose(2, 1, 0)),
        "wg": con(np.asarray(L0_ffn_w_gate).T),
        "wu": con(np.asarray(L0_ffn_w_up).T),
        "wd": con(np.asarray(L0_ffn_w_down).T),
        "qln": con(np.asarray(L0_attn_q_a_ln_w).reshape(QR, 1)),
        "kvln": con(L0_attn_kv_a_ln_w),
        "cT": con(np.asarray(L0_c).T.reshape(KC, P, B).transpose(1, 0, 2).reshape(P, KC * B)),
        "wmod": con(L0_wmod),
        "cos": cos,
        "sin2": sin2,
    }
    nc = bacc.Bacc("TRN2", target_bir_lowering=False, num_devices=1)
    aps = {n: nc.dram_tensor(n, a.shape, F32, kind="ExternalInput").ap() for n, a in arrays.items()}
    out = nc.dram_tensor("out", (B, S, D), F32, kind="ExternalOutput").ap()
    mod_dram = nc.dram_tensor("mod_dram", (B, 6 * D), F32, kind="Internal").ap()
    adaln_block(nc, *aps.values(), out, mod_dram)
    r = run_bass_kernel_spmd(nc, [arrays], core_ids=[0])
    return r.results[0]["out"]
```

```python
from contextlib import ExitStack

import concourse.bass as bass
from concourse import mybir

F32 = mybir.dt.float32
F32R = mybir.dt.float32r
I32 = mybir.dt.int32
BF16 = mybir.dt.bfloat16
ALU = mybir.AluOpType
ACT = mybir.ActivationFunctionType
AX = mybir.AxisListType

P = 128
B, S, D = 4, 512, 512
H, NOPE, ROPE, VD, KVR, QR = 32, 64, 64, 128, 32, 128
HALF = ROPE // 2
I = 1376
TC = S // P
KC = D // P
IC = (I + P - 1) // P
HG = 4
G = H // HG
QD = KVR + ROPE
QW = HG * QD
QA = QR + KVR + ROPE
TRI = P * TC * (TC + 1) // 2
ONE = 1
NEG = -3.0e38
EPS_LN, EPS_RMS, EPS_BIT = 1e-5, 1e-6, 1e-5
MSCALE = 0.1 * 4.852030263919617 + 1.0
SCALE = (NOPE + ROPE) ** -0.5 * MSCALE * MSCALE

SC_ORDER = [3, 2, 0, 1]
SC_BANK = {3: (0, 0), 2: (1, 0), 0: (1, 384), 1: (0, 0)}
P_OFF = {3: 0, 2: 512, 0: 896, 1: 1024}
T_OFF = {0: 0, 1: 512, 3: 896, 2: 1024}
ACT_COLS = 1024


DVE_AFTER = {0: 0, 1: 1, 2: 2, 5: 3, 6: 4}


def rows_of(ic):
    return min(P, I - ic * P)


def adaln_block(nc, x, wa, wqn, wkn, wqp, wv, wo, wg, wu, wd, qln, kvln, cT, wmod, cos, sin2, out, mod_dram):
    top = [(nc.sbuf_base + 31) // 32 * 32]

    def place(name, shape, dt=F32, at=None):
        size = 4
        for n in shape[1:]:
            size *= n
        off = top[0] if at is None else at
        t = nc.alloc_sbuf_tensor_at(name, list(shape), dt, offset=off)
        end = (off + size + 31) // 32 * 32
        assert end <= nc.sbuf_usable_end, name
        if at is None:
            top[0] = end
        return t, end

    ident, _ = place("ident", (P, P))
    ones, _ = place("ones", (P, P))
    mask, _ = place("mask", (P, S))
    cos_sb, _ = place("cos_sb", (P, TC, HALF))
    sin_sb, _ = place("sin_sb", (P, TC, 2, HALF))
    junk, _ = place("junk", (P, IC * D // 4 // 2), at=top[0])
    g_sb, _ = place("g_sb", (P, G, D))
    wq_sb, _ = place("wq_sb", (P, G * QW))
    wa_sb, _ = place("wa_sb", (P, KC, QA))
    kvln_sb, _ = place("kvln_sb", (P, KVR))
    qln_sb, _ = place("qln_sb", (P, 1))
    gate_raw, _ = place("gate_raw", (P, KC, I), at=top[0])
    gate_w, _ = place("gate_w", (P, KC, I), F32R)
    up_raw, _ = place("up_raw", (P, KC, I), at=top[0])
    up_w, _ = place("up_w", (P, KC, I), F32R)
    down_raw, _ = place("down_raw", (P, IC, D), at=top[0])
    down_w, _ = place("down_w", (P, IC, D), F32R)
    bit, _ = place("bit", (P, 32))
    mod_all, _ = place("mod_all", (P, 4, KC, B))
    x_sb, _ = place("x_sb", (P, TC, D))
    wqn_t, _ = place("wqn_t", (NOPE, H, QR), at=top[0])
    ut_sb, _ = place("ut_sb", (P, TC, 2 * D))
    wv_t, _ = place("wv_t", (P, H, KVR), at=top[0])
    ga_sb, _ = place("ga_sb", (P, D))
    gb_sb, _ = place("gb_sb", (P, D))
    mod_a, _ = place("mod_a", (P, 2, KC))
    mod_c, _ = place("mod_c", (P, 2, KC))
    qnT, _ = place("qnT", (P, S))
    kt_sb, _ = place("kt_sb", (P, TC, QD))
    wkn_t, _ = place("wkn_t", (NOPE, H, KVR), at=top[0])
    k_hi, _ = place("k_hi", (P, S), F32R)
    k_lo, _ = place("k_lo", (P, S), F32R)
    small_a, _ = place("small_a", (P, 96))
    small_c, _ = place("small_c", (P, 96))
    shared = top[0]
    qs, e = place("qs", (P, 2, TC, HG, QD), at=shared)
    q_hi, e = place("q_hi", (P, 2, S), F32R, at=e)
    q_lo, e = place("q_lo", (P, 2, S), F32R, at=e)
    pr, e = place("pr", (P, 2, TRI), at=e)
    pts, e = place("pts", (P, HG, TRI), at=e)
    rot, e = place("rot", (P, 2, 2, 2, HG, HALF), at=e)
    rb, e = place("rb", (P, 2, TC, HG, KVR), at=e)
    rsb, e = place("rsb", (P, S), at=e)
    stat, e = place("stat", (P, 64), at=e)
    xn, e = place("xn", (P, TC, D), at=shared)
    h2, e = place("h2", (P, KC, S), at=e)
    xn_a, hT = xn, h2
    stage, _ = place("stage", (P, 2, KC, 2 * D), at=e)
    h2_hi, e = place("h2_hi", (P, KC, S), F32R, at=e)
    h2_lo, e = place("h2_lo", (P, KC, S), F32R, at=e)
    gcopy, e = place("gcopy", (P, 2, S), at=e)
    inter, e = place("inter", (P, 2, S), at=e)
    i_hi, e = place("i_hi", (P, 2, S), F32R, at=e)
    i_lo, e = place("i_lo", (P, 2, S), F32R, at=e)
    qa_sb, e = place("qa_sb", (P, TC, QA), at=e)
    qtok, e = place("qtok", (P, TC, QR), at=e)
    scr, e = place("scr", (P, TC, QR), at=e)
    krot, e = place("krot", (P, 2, TC, 2, HALF), at=e)
    mrow, _ = place("mrow", (B, 6, D), at=e)
    below, e = place("below", (P, 2, IC * D // 4), at=shared)
    wv_all = wv_t[:]
    c_t, ce_t, cs_t = small_c[:, 0:16], small_c[:, 16:32], small_c[:, 32:48]

    ctx = ExitStack()
    ps = ctx.enter_context(nc.psum_tensor("ps", [P, 8, 512], F32))

    def sem(name):
        return ctx.enter_context(nc.semaphore(name))

    su_w = [sem(f"su_w{i}") for i in range(3)]
    su_stage = [sem(f"su_stage{i}") for i in range(2)]
    su_const = sem("su_const")
    su_c = sem("su_c")
    su_qk = sem("su_qk")
    su_wqp = sem("su_wqp")
    su_wv = sem("su_wv")
    su_wa = sem("su_wa")
    su_id = sem("su_id")
    su_exp = sem("su_exp")
    su_silu = sem("su_silu")
    su_modps = sem("su_modps")
    su_modsb = sem("su_modsb")
    su_gate = sem("su_gate")
    su_gst = sem("su_gst")
    su_mt = sem("su_mt")
    su_wqps = sem("su_wqps")
    su_wqsb = sem("su_wqsb")
    su_gps = sem("su_gps")
    su_gsb = sem("su_gsb")
    su_sum = sem("su_sum")
    su_sumps = sem("su_sumps")
    su_bit = sem("su_bit")
    su_pad = sem("su_pad")
    su_modall = sem("su_modall")

    waits_passed = sem("waits_passed")
    x_in = sem("x_in")
    ga_in = sem("ga_in")
    gb_in = sem("gb_in")
    moda_done = sem("moda_done")
    modc_done = sem("modc_done")
    x2_done = sem("x2_done")
    y_done = sem("y_done")
    y_out = sem("y_out")
    chain_a = sem("chain_a")
    chain_c = sem("chain_c")
    xa_done = sem("xa_done")
    xc_done = sem("xc_done")
    tra_done = sem("tra_done")
    trc_done = sem("trc_done")
    hT_done = sem("hT_done")
    h2_done = sem("h2_done")
    qa_ps = sem("qa_ps")
    qa_done = sem("qa_done")
    tok_done = sem("tok_done")
    lat_tr = sem("lat_tr")
    qnT_done = sem("qnT_done")
    kh_done = sem("kh_done")
    kl_done = sem("kl_done")
    qg_done = sem("qg_done")
    qg_abs = sem("qg_abs")
    qg_rot = sem("qg_rot")
    qs_done = sem("qs_done")
    q_tr = sem("q_tr")
    qh_done = sem("qh_done")
    ql_done = sem("ql_done")
    s_done = sem("s_done")
    s_red = sem("s_red")
    negm = sem("negm")
    p_done = sem("p_done")
    pt_done = sem("pt_done")
    pts_act = sem("pts_act")
    pts_dve = sem("pts_dve")
    rs_done = sem("rs_done")
    rb_done = sem("rb_done")
    av_done = sem("av_done")
    r_done = sem("r_done")
    rsb_done = sem("rsb_done")
    ut_done = sem("ut_done")
    op_done = sem("op_done")
    h2hi_done = sem("h2hi_done")
    h2lo_done = sem("h2lo_done")
    gate_ps = sem("gate_ps")
    up_ps = sem("up_ps")
    gc_done = sem("gc_done")
    in_done = sem("in_done")
    ihi_done = sem("ihi_done")
    ilo_done = sem("ilo_done")
    dn_used = sem("dn_used")
    dn_done = sem("dn_done")

    from_one = [x2_done, y_done, y_out, s_done, av_done, pts_act, pts_dve, rsb_done, qg_abs, qg_rot, qh_done,
                ql_done, s_red, ut_done, q_tr, in_done]

    def alone(eng):
        eng.sem_inc(waits_passed, 1)

    x_v = x.rearrange("b (t p) d -> b p t d", p=P)
    out_v = out.rearrange("b (t p) d -> b p t d", p=P)
    N_CHAIN_A, N_CHAIN_C = 50, 64

    def rsqrt(dve, link, linked, y, v, a, t, eps):
        link(dve.tensor_scalar(a, v, eps, None, ALU.add))
        linked()
        link(dve.tensor_scalar(t.bitcast(I32), a.bitcast(I32), 1, None, ALU.logical_shift_right))
        linked()
        link(dve.tensor_scalar(y.bitcast(I32), t.bitcast(I32), -1.0, float(0x5f3759df), ALU.mult, ALU.add))
        linked()
        for _ in range(3):
            link(dve.tensor_tensor(t, y, y, ALU.mult))
            linked()
            link(dve.scalar_tensor_tensor(t, t, -0.5, a, ALU.mult, ALU.mult))
            linked()
            link(dve.scalar_tensor_tensor(y, t, 1.5, y, ALU.add, ALU.mult))
            linked()

    def linker(eng, chain, base):
        n = [0]

        def link(ins):
            n[0] += 1
            ins.then_inc(chain, 1)

        def linked():
            eng.wait_ge(chain, base + n[0])
        return n, link, linked

    def pe_rows(pe, bb, half, pair):
        pe.wait_ge(xa_done, (bb + 1) * TC)
        for k in range(2 * half, 2 * half + 2):
            for t in range(TC):
                m = pe.transpose(ps[:, pair + k % 2, t * P:(t + 1) * P], xn_a[:, t, k * P:(k + 1) * P], ident[:])
            m.then_inc(tra_done, 1)

    def pe_latents(pe, bb, pair):
        pe.wait_ge(hT_done, (bb + 1) * KC)
        for t in range(TC):
            for k in range(KC):
                m = pe.matmul(ps[:, pair + t // 2, (t % 2) * 256:(t % 2) * 256 + QA], hT[:, k, t * P:(t + 1) * P],
                              wa_sb[:, k, :], start=(k == 0), stop=(k == KC - 1))
        m.then_inc(qa_ps, 1)

    def pe_latents_t(pe, bb, pair):
        pe.wait_ge(tok_done, (bb + 1) * 2)
        for t in range(TC):
            m = pe.transpose(ps[:, pair, t * P:(t + 1) * P], qtok[:, t, :], ident[:])
        m.then_inc(lat_tr, 1)
        for t in range(TC):
            m = pe.transpose(ps[0:QD, pair + 1, t * P:(t + 1) * P], kt_sb[:, t, :], ident[:])
        m.then_inc(lat_tr, 1)

    def act_rows(act, bb, half, pair):
        if half == 0:
            act.wait_ge(moda_done, bb + 1)
        for k in range(2 * half, 2 * half + 2):
            act.wait_ge(tra_done, bb * KC + k + 1)
            act.activation(hT[:, k, :], ps[:, pair + k % 2, :], ACT.Identity, bias=mod_a[:, 0, k:k + 1],
                           scale=mod_a[:, 1, k:k + 1]).then_inc(hT_done, 1)

    def act_latents(act, bb, pair):
        act.wait_ge(qa_ps, bb + 1)
        act.activation(qa_sb[:].rearrange("p (a t) n -> p a t n", a=2),
                       ps[:, pair:pair + 2, :].rearrange("p a (t n) -> p a t n", t=2)[:, :, :, 0:QA],
                       ACT.Copy).then_inc(qa_done, 1)

    def act_latents_t(act, bb, pair):
        act.wait_ge(lat_tr, bb * 2 + 1)
        act.activation(qnT[:], ps[:, pair, :], ACT.Copy, scale=qln_sb[:, 0:1]).then_inc(qnT_done, 1)
        act.wait_ge(lat_tr, bb * 2 + 2)
        act.activation(k_hi[0:QD, :], ps[0:QD, pair + 1, :], ACT.Copy).then_inc(kh_done, 1)

    def dve_projections(dve, bb):
        n, link, linked = linker(dve, chain_a, bb * N_CHAIN_A)
        mv = small_a[:, 24:32].rearrange("p (t e) -> p t e", e=2)

        def statistics():
            dve.tensor_copy(mod_a[:], mod_all[:, 0:2, :, bb]).then_inc(moda_done, 1)
            dve.wait_ge(x_in, (bb + 1) * 16)
            for t in range(TC):
                link(dve.bn_stats(small_a[:, 6 * t:6 * t + 6], x_sb[:, t, :]))

        def root():
            linked()
            alone(dve)
            for t in range(TC):
                link(dve.bn_aggr(small_a[:, 24 + 2 * t:26 + 2 * t], small_a[:, 6 * t:6 * t + 6]))
            linked()
            rsqrt(dve, link, linked, small_a[:, 32:36], mv[:, :, 1], small_a[:, 64:68], small_a[:, 72:76], EPS_LN)

        def rows():
            for t in range(TC):
                dve.tensor_scalar(xn_a[:, t, :], x_sb[:, t, :], small_a[:, 24 + 2 * t:25 + 2 * t],
                                  small_a[:, 32 + t:33 + t], ALU.subtract, ALU.mult).then_inc(xa_done, 1)

        def norms():
            dve.wait_ge(qa_done, bb + 1)
            for t in range(TC):
                link(dve.tensor_tensor_reduce(scr[:, t, :], qa_sb[:, t, 0:QR], qa_sb[:, t, 0:QR], 1.0 / QR, 0.0,
                                              ALU.mult, ALU.add, small_a[:, 40 + t:41 + t]))
                link(dve.tensor_tensor_reduce(krot[:, 0, t, 0, :], qa_sb[:, t, QR:QR + KVR],
                                              qa_sb[:, t, QR:QR + KVR], 1.0 / KVR, 0.0,
                                              ALU.mult, ALU.add, small_a[:, 44 + t:45 + t]))
            linked()
            rsqrt(dve, link, linked, small_a[:, 48:56], small_a[:, 40:48], small_a[:, 64:72], small_a[:, 72:80],
                  EPS_RMS)

        def latents():
            for t in range(TC):
                link(dve.tensor_scalar(qtok[:, t, :], qa_sb[:, t, 0:QR], small_a[:, 48 + t:49 + t], None, ALU.mult))
                link(dve.scalar_tensor_tensor(kt_sb[:, t, 0:KVR], qa_sb[:, t, QR:QR + KVR],
                                              small_a[:, 52 + t:53 + t], kvln_sb[:], ALU.mult, ALU.mult))
            xk = qa_sb[:, :, QR + KVR:QA].rearrange("p t (e j) -> p t e j", e=2)
            link(dve.tensor_tensor(krot[:, 0], xk, cos_sb[:].unsqueeze(2).broadcast_to((P, TC, 2, HALF)), ALU.mult))
            link(dve.tensor_tensor(krot[:, 1], xk, sin_sb[:], ALU.mult))
            linked()
            dve.tensor_tensor(kt_sb[:, :, KVR:KVR + HALF], krot[:, 0, :, 0], krot[:, 1, :, 1],
                              ALU.add).then_inc(tok_done, 1)
            dve.tensor_tensor(kt_sb[:, :, KVR + HALF:QD], krot[:, 0, :, 1], krot[:, 1, :, 0],
                              ALU.add).then_inc(tok_done, 1)
            assert n[0] == N_CHAIN_A, n[0]

        return [statistics, root, rows, norms, latents]

    def dve_key_low(dve, bb, pair):
        dve.wait_ge(kh_done, bb + 1)
        dve.tensor_tensor(k_lo[0:QD, :], ps[0:QD, pair + 1, :], k_hi[0:QD, :].bitcast(F32),
                          ALU.subtract).then_inc(kl_done, 1)

    with nc.Block() as block:
        @block.sync
        def _(sp):
            for s_ in from_one:
                sp.sem_inc(s_, ONE)
            sp.dma_start(c_t, cT).then_inc(su_c, 16)
            sp.dma_start(gate_raw[:], wg.rearrange("(k p) n -> p k n", p=P)).then_inc(su_w[0], 16)
            sp.dma_start(wqn_t[:], wqn).then_inc(su_qk, 16)
            sp.dma_start(wkn_t[:], wkn).then_inc(su_qk, 16)
            wmod_v = wmod.rearrange("(k p) n -> p k n", p=P)
            for i in range(2):
                sp.dma_start(stage[:, i % 2], wmod_v[:, :, i * 1024:(i + 1) * 1024]).then_inc(su_stage[i % 2], 16)
            sp.dma_start(x_sb[:], x_v[0]).then_inc(x_in, 16)
            sp.dma_start(up_raw[:], wu.rearrange("(k p) n -> p k n", p=P)).then_inc(su_w[1], 16)
            sp.wait_ge(su_modps, 2)
            sp.dma_start(stage[:, 0], wmod_v[:, :, 2048:3072]).then_inc(su_stage[0], 16)
            sp.dma_start(wa_sb[:], wa.rearrange("(k p) n -> p k n", p=P)).then_inc(su_wa, 16)
            sp.dma_start(cos_sb[:], cos.rearrange("(t p) j -> p t j", p=P)).then_inc(su_const, 16)
            sp.dma_start(sin_sb[:], sin2.rearrange("(t p) e j -> p t e j", p=P)).then_inc(su_const, 16)
            sp.dma_start(qln_sb[:], qln).then_inc(su_const, 16)
            sp.dma_start(kvln_sb[:], kvln.partition_broadcast(P)).then_inc(su_const, 16)
            sp.wait_ge(su_pad, 1)
            sp.dma_start(down_raw[:, 0:IC - 1, :],
                         wd[0:(IC - 1) * P, :].rearrange("(k p) n -> p k n", p=P)).then_inc(su_w[2], 16)
            sp.dma_start(down_raw[0:rows_of(IC - 1), IC - 1, :], wd[(IC - 1) * P:, :]).then_inc(su_w[2], 16)
            sp.dma_start(wq_sb[:].rearrange("p (g a n) -> p g a n", g=G, a=3)[:, :, 1:3, :], wqp).then_inc(su_wqp, 16)
            sp.dma_start(wv_all, wv).then_inc(su_wv, 16)
            for i in range(4):
                if i == 0:
                    sp.wait_ge(su_modps, 6)
                if i >= 2:
                    sp.wait_ge(su_gps, 2 * (i - 1))
                sp.dma_start(stage[:, i % 2].rearrange("p k n -> p (k n)").rearrange("p (h n) -> p h n", h=8),
                             wo[:, i * 8:(i + 1) * 8, :]).then_inc(su_stage[i % 2], 16)
            sp.wait_ge(su_gate, 4)
            sp.dma_start(mod_dram, mrow[:]).then_inc(su_gst, 16)
            sp.wait_ge(su_gst, 16)
            sp.wait_ge(su_wqp, 16)
            sp.wait_ge(su_gps, G)
            sp.dma_start(ga_sb[:], mod_dram[0, 2 * D:3 * D].partition_broadcast(P)).then_inc(ga_in, 16)
            sp.dma_start(gb_sb[:], mod_dram[0, 5 * D:6 * D].partition_broadcast(P)).then_inc(gb_in, 16)

        @block.gpsimd
        def _(pool):
            pool.memset(ident[:], 0.0).then_inc(su_id, 1)
            pool.memset(ones[:], 1.0).then_inc(su_id, 1)
            pool.memset(mask[:], 0.0).then_inc(su_id, 1)
            pool.memset(down_raw[:, IC - 1, :], 0.0).then_inc(su_pad, 1)
            pool.wait_ge(su_id, 3)
            pool.affine_select(out=ident[:], in_=ident[:], compare_op=ALU.not_equal, fill=1.0, base=0,
                               pattern=[[-1, P]], channel_multiplier=1).then_inc(su_id, 1)
            pool.affine_select(out=mask[:], in_=mask[:], compare_op=ALU.is_ge, fill=NEG, base=S - P,
                               pattern=[[-1, S]], channel_multiplier=1).then_inc(su_id, 1)

        @block.scalar
        def _(act):
            act.wait_ge(su_c, 16)
            act.activation(ce_t, c_t, ACT.Exp, scale=-1.0).then_inc(su_exp, 1)

            def sums(n, raw, need):
                act.wait_ge(su_w[n], need)
                flat = raw[:].rearrange("p a b -> p (a b)")
                q = flat.shape[1] // 4
                for i in range(4):
                    if 4 * n + i >= 1:
                        act.wait_ge(su_sum, 4 * n + i)
                    act.activation(junk[:].bitcast(BF16)[:, 0:q], flat[:, i * q:(i + 1) * q], ACT.Abs,
                                   accum_out=bit[:, 4 * n + i:4 * n + i + 1]).then_inc(su_sum, 1)

            sums(0, gate_raw, 16)
            for i in range(2):
                act.wait_ge(su_wqps, i + 1)
                act.activation(wq_sb[:].rearrange("p (g a n) -> p g a n", g=G, a=3)[:, 4 * i:4 * i + 4, 0, :],
                               ps[:, 2 + i, :].rearrange("p (g n) -> p g n", g=4), ACT.Copy).then_inc(su_wqsb, 1)
            sums(1, up_raw, 16)
            act_rows(act, 0, 0, 4)
            act_rows(act, 0, 1, 6)
            act_latents(act, 0, 4)
            sums(2, down_raw, 32)
            act.wait_ge(su_const, 64)
            act_latents_t(act, 0, 6)
            for g in range(G):
                act.wait_ge(su_gps, g + 1)
                act.activation(g_sb[:, g, :], ps[:, g % 2, :], ACT.Copy).then_inc(su_gsb, 1)

        @block.tensor
        def _(pe):
            pe.wait_ge(su_qk, 32)
            for h in range(H):
                m = pe.matmul(ps[:, 2 + h // 16, (h % 16) * KVR:(h % 16 + 1) * KVR], wqn_t[:, h, :], wkn_t[:, h, :],
                              start=True, stop=True)
                if h % 16 == 15:
                    m.then_inc(su_wqps, 1)
            pe.wait_ge(su_silu, 3)
            for i in range(3):
                pe.wait_ge(su_stage[i % 2], 16 * (i // 2 + 1))
                for n in range(2):
                    if 2 * i + n >= 2:
                        pe.wait_ge(su_modsb, 2 * i + n - 1)
                    for k in range(KC):
                        m = pe.matmul(ps[0:B, n, :], cs_t[:, k * B:(k + 1) * B], stage[:, i % 2, k, n * D:(n + 1) * D],
                                      start=(k == 0), stop=(k == KC - 1))
                    m.then_inc(su_modps, 1)
            pe.wait_ge(su_modsb, 6)
            pe.wait_ge(su_wqsb, 1)
            pe.wait_ge(su_id, 5)
            for n, a in enumerate((0, 1, 3, 4)):
                for k in range(KC):
                    i = (n * KC + k) * B
                    m = pe.transpose(ps[:, 2, i:i + B], mrow[:, a, k * P:(k + 1) * P], ident[0:B, 0:B])
            m.then_inc(su_mt, 1)
            pe_rows(pe, 0, 0, 4)
            pe_rows(pe, 0, 1, 6)
            pe.wait_ge(su_wa, 16)
            pe_latents(pe, 0, 4)
            pe.wait_ge(hT_done, KC)
            pe_latents_t(pe, 0, 6)
            pe.wait_ge(su_sum, 12)
            pe.wait_ge(su_modall, 1)
            pe.matmul(ps[:, 2, 0:12], ones[:], bit[:, 0:12], start=True, stop=True).then_inc(su_sumps, 1)
            pe.wait_ge(su_wv, 16)
            for g in range(G):
                i = g // 2
                pe.wait_ge(su_stage[i % 2], 16 * ((2 if i % 2 == 0 else 1) + i // 2 + 1))
                if g >= 2:
                    pe.wait_ge(su_gsb, g - 1)
                for j in range(HG):
                    h = g * HG + j
                    m = pe.matmul(ps[j * KVR:(j + 1) * KVR, g % 2, :], wv_all[:, h, :],
                                  stage[:, i % 2].rearrange("p k n -> p (k n)")[:, (h % 8) * D:(h % 8 + 1) * D],
                                  start=True, stop=True)
                m.then_inc(su_gps, 1)

        @block.vector
        def _(dve):
            dve.wait_ge(su_exp, 1)
            dve.tensor_scalar(ce_t, ce_t, 1.0, None, ALU.add).then_inc(su_silu, 1)
            dve.wait_ge(su_silu, 1)
            dve.reciprocal(cs_t, ce_t).then_inc(su_silu, 1)
            dve.wait_ge(su_silu, 2)
            dve.tensor_tensor(cs_t, cs_t, c_t, ALU.mult).then_inc(su_silu, 1)
            for i in range(6):
                dve.wait_ge(su_modps, i + 1)
                dve.tensor_copy(mrow[:, i, :], ps[0:B, i % 2, :]).then_inc(su_modsb, 1)
            dve.wait_ge(su_mt, 1)
            dve.tensor_copy(mod_all[:].rearrange("p a k b -> p (a k b)"), ps[:, 2, 0:4 * KC * B]).then_inc(su_modall, 1)
            dve.wait_ge(su_modall, 1)
            scales = mod_all[:].rearrange("p (e f) k b -> p e f (k b)", f=2)[:, :, 1, :]
            dve.tensor_scalar(scales, scales, 1.0, None, ALU.add).then_inc(su_modall, 1)
            dve.wait_ge(su_modall, 2)
            statistics, root, rows, norms, latents = dve_projections(dve, 0)
            statistics()
            root()
            rows()
            gates = mrow[:].rearrange("b (e f) n -> b e f n", e=2)[:, :, 2, :]
            size = mrow[:].rearrange("b (e f) n -> b e f n", e=2)[:, :, 0, :]
            dve.scalar_tensor_tensor(size, gates, -1.0, gates, ALU.mult, ALU.max).then_inc(su_gate, 1)
            dve.wait_ge(su_gate, 1)
            dve.tensor_scalar(gates, gates, 0.0, 2.0, ALU.is_ge, ALU.mult).then_inc(su_gate, 1)
            dve.wait_ge(su_gate, 2)
            dve.tensor_scalar(gates, gates, -1.0, None, ALU.add).then_inc(su_gate, 1)
            dve.wait_ge(su_gate, 3)
            dve.scalar_tensor_tensor(gates, size, 0.25, gates, ALU.max, ALU.mult).then_inc(su_gate, 1)
            norms()
            dve.wait_ge(su_const, 64)
            latents()
            dve_key_low(dve, 0, 6)
            dve.wait_ge(su_sumps, 1)
            dve.tensor_reduce(bit[:, 12:15], ps[:, 2, 0:12].rearrange("p (n i) -> p n i", n=3), AX.X,
                              ALU.add).then_inc(su_bit, 1)
            dve.wait_ge(su_bit, 1)
            dve.tensor_scalar(bit[:, 15:18], bit[:, 12:15], 1.0 / (I * D), None, ALU.mult).then_inc(su_bit, 1)
            dve.wait_ge(su_bit, 2)
            dve.tensor_scalar(bit[:, 18:21], bit[:, 15:18], EPS_BIT, 0.5, ALU.add, ALU.mult).then_inc(su_bit, 1)
            dve.tensor_tensor(bit[:, 24:25], bit[:, 15:16], bit[:, 16:17], ALU.mult).then_inc(su_bit, 1)
            dve.wait_ge(su_bit, 4)
            dve.tensor_tensor(bit[:, 25:26], bit[:, 24:25], bit[:, 17:18], ALU.mult).then_inc(su_bit, 1)
            dve.tensor_scalar(bit[:, 21:24], bit[:, 18:21], -1.0, None, ALU.mult).then_inc(su_bit, 1)
            dve.wait_ge(su_bit, 6)
            n_bit = 6
            for n, (raw, w) in enumerate(((gate_raw, gate_w), (up_raw, up_w), (down_raw, down_w))):
                rf, wf = (a[:].rearrange("p a b -> p (a b)") for a in (raw, w))
                q = rf.shape[1] // 4
                for i in range(4):
                    sl = slice(i * q, (i + 1) * q)
                    b_ = below[:, i % 2, 0:q]
                    dve.tensor_scalar(b_, rf[:, sl], bit[:, 21 + n:22 + n], None, ALU.is_lt).then_inc(su_bit, 1)
                    n_bit += 1
                    dve.wait_ge(su_bit, n_bit)
                    dve.scalar_tensor_tensor(wf[:, sl], rf[:, sl], bit[:, 18 + n:19 + n], b_, ALU.is_gt,
                                             ALU.subtract).then_inc(su_bit, 1)
                    n_bit += 1
            dve.wait_ge(su_bit, n_bit)

    def steps(eng, b, step):
        with eng.Fori(0, H // 8 - 1) as it:
            for j in range(8):
                step(b * H + it * 8, b * G + it * 2, it * 2, j, False)
        it = H // 8 - 1
        for j in range(8):
            step(b * H + it * 8, b * G + it * 2, it * 2, j, True)

    def batches(eng, batch):
        with eng.Fori(0, B - 1) as b:
            batch(b, True)
        batch(B - 1, False)

    def ffn_order(with_next):
        if not with_next:
            return [("F", ic) for ic in range(IC)]
        return ([("F", 0), ("F", 1), ("F", 2), ("F", 3), ("R", 0), ("R", 1), ("F", 4), ("F", 5), ("L", 0), ("F", 6),
                 ("F", 7), ("F", 8), ("T", 0)] + [("F", ic) for ic in range(9, IC)])

    with nc.Block() as block:
        @block.sync
        def _(sp):
            def batch(b, with_next):
                if with_next:
                    sp.wait_ge(x2_done, ONE + (b + 1) * TC)
                    alone(sp)
                    sp.dma_start(x_sb[:], x_v[b + 1]).then_inc(x_in, 16)
                    sp.dma_start(ga_sb[:], mod_dram[b + 1, 2 * D:3 * D].partition_broadcast(P)).then_inc(ga_in, 16)
                for t in range(TC):
                    sp.wait_ge(y_done, ONE + b * TC + t + 1)
                    alone(sp)
                    sp.dma_start(out_v[b, :, t, :], ut_sb[:, t, 0:D]).then_inc(y_out, 16)
                if with_next:
                    sp.dma_start(gb_sb[:], mod_dram[b + 1, 5 * D:6 * D].partition_broadcast(P)).then_inc(gb_in, 16)
            batches(sp, batch)
            sp.wait_ge(y_out, ONE + B * 16 * TC)

        @block.gpsimd
        def _(pool):
            def rotate(pb, p, G_par, tc, first):
                pool.wait_ge(qg_rot, ONE + (pb + p + 1) * 2)
                if not first:
                    pool.wait_ge(q_tr, ONE + pb + 4 * (p // 4 - 1))
                r = rot[:, p % 2]
                o = qs[:, G_par, tc]
                pool.tensor_tensor(o[:, :, KVR:KVR + HALF], r[:, 0, 0], r[:, 1, 1], ALU.add).then_inc(qs_done, 1)
                pool.tensor_tensor(o[:, :, KVR + HALF:QD], r[:, 0, 1], r[:, 1, 0], ALU.add).then_inc(qs_done, 1)

            def batch(b, with_next):
                for p in range(7):
                    rotate(b * H, p, p // 4, p % 4, p < 4)

                def step(ub, gb, gl, j, last):
                    pool.wait_ge(rs_done, ub + j + 1)
                    alone(pool)
                    pool.tensor_copy(rb[:, j // 4, :, j % 4, :],
                                     stat[:, 32 + 4 * (j % 4):36 + 4 * (j % 4)].unsqueeze(2).broadcast_to((P, TC, KVR))
                                     ).then_inc(rb_done, 1)
                    p = j + 7
                    if not (last and p >= 8):
                        rotate(ub, p, (p // 4) % 2, p % 4, False)
                steps(pool, b, step)
            batches(pool, batch)

        @block.scalar
        def _(act):
            def q_abs(ub, p, first):
                act.wait_ge(qg_rot, ONE + (ub + p + 1) * 2)
                if not first:
                    act.wait_ge(q_tr, ONE + ub + 4 * (p // 4 - 1))
                act.activation(qs[:, (p // 4) % 2, p % 4, :, 0:KVR],
                               ps[:, 7, 0:HG * KVR].rearrange("p (h c) -> p h c", h=HG), ACT.Copy).then_inc(qg_abs, 1)

            def q_high(ub, v):
                act.wait_ge(q_tr, ONE + ub + v + 1)
                if v >= 1:
                    act.wait_ge(s_done, ONE + (ub + v - 1) * 4)
                act.activation(q_hi[0:QD, v % 2, :], ps[0:QD, 5, :], ACT.Copy).then_inc(qh_done, 1)

            def exps(ub, x_):
                act.wait_ge(negm, ub + x_ + 1)
                for i, qc in enumerate(SC_ORDER):
                    n = (qc + 1) * P
                    pp = pr[:, x_ % 2, P_OFF[qc]:P_OFF[qc] + n]
                    m = act.activation(pp, pp, ACT.Exp, bias=stat[:, 8 + 4 * (x_ % 2) + qc:9 + 4 * (x_ % 2) + qc],
                                       scale=SCALE, accum_out=stat[:, 16 + 4 * (x_ % 4) + qc:17 + 4 * (x_ % 4) + qc])
                m.then_inc(p_done, 1)

            def batch(b, with_next):
                for p in range(4):
                    q_abs(b * H, p, True)
                q_high(b * H, 0)
                for p in range(4, 7):
                    q_abs(b * H, p, False)
                q_high(b * H, 1)
                exps(b * H, 0)
                q_high(b * H, 2)

                def step(ub, gb, gl, j, last):
                    g = j // 4
                    if not (last and j + 1 >= 8):
                        exps(ub, j + 1)
                    act.wait_ge(pt_done, ub + j + 1)
                    act.wait_ge(av_done, ONE + gb + g)
                    act.activation(pts[:, j % 4, 0:ACT_COLS],
                                   ps[:, 2:5, :].rearrange("p a n -> p (a n)")[:, 0:ACT_COLS],
                                   ACT.Copy).then_inc(pts_act, 1)
                    if not (last and j + 3 >= 8):
                        q_high(ub, j + 3)
                    if j % 4 == 3:
                        act.wait_ge(r_done, gb + g + 1)
                        act.activation(rsb[:], ps[:, 6, :], ACT.Copy).then_inc(rsb_done, 1)
                    if not (last and j + 7 >= 8):
                        q_abs(ub, j + 7, False)
                steps(act, b, step)

                act.wait_ge(modc_done, b + 1)
                for t in range(TC):
                    act.wait_ge(trc_done, b * TC + t + 1)
                    cols = slice(t * P, (t + 1) * P)
                    for k in range(KC):
                        m = act.activation(h2[:, k, cols], ps[:, 4 + t % 2, k * P:(k + 1) * P], ACT.Identity,
                                           bias=mod_c[:, 0, k:k + 1], scale=mod_c[:, 1, k:k + 1])
                    m.then_inc(h2_done, 1)
                    act.wait_ge(h2_done, b * TC + t + 1)
                    act.activation(h2_hi[:, :, cols], h2[:, :, cols], ACT.Copy).then_inc(h2hi_done, 1)

                for n, (kind, ic) in enumerate(ffn_order(with_next)):
                    pair = 4 + 2 * (n % 2)
                    if kind == "R":
                        act_rows(act, b + 1, ic, pair)
                        continue
                    if kind == "L":
                        act_latents(act, b + 1, pair)
                        continue
                    if kind == "T":
                        act_latents_t(act, b + 1, pair)
                        continue
                    M = rows_of(ic)
                    act.wait_ge(gate_ps, b * IC + ic + 1)
                    if ic >= 2:
                        act.wait_ge(in_done, ONE + b * IC + ic - 1)
                    act.activation(gcopy[0:M, ic % 2, :], ps[0:M, pair, :], ACT.Copy).then_inc(gc_done, 1)
                    act.wait_ge(in_done, ONE + b * IC + ic + 1)
                    if ic >= 2:
                        act.wait_ge(dn_used, b * (IC - 1) + ic - 1)
                    act.activation(i_hi[0:M, ic % 2, :], inter[0:M, ic % 2, :], ACT.Copy).then_inc(ihi_done, 1)
            batches(act, batch)

        @block.tensor
        def _(pe):
            def q_gen(ub, p, gl):
                pe.wait_ge(qg_abs, ONE + ub + p)
                pe.wait_ge(qg_rot, ONE + (ub + p) * 2)
                tc = p % 4
                w = wq_sb[:, bass.ds((gl + p // 4) * QW, QW)]
                pe.matmul(ps[:, 7, 0:QW], qnT[:, tc * P:(tc + 1) * P], w, start=True, stop=True).then_inc(qg_done, 1)

            def q_transpose(ub, v):
                pe.wait_ge(qs_done, (ub + 4 * (v // 4) + 4) * 2)
                pe.wait_ge(qg_abs, ONE + ub + 4 * (v // 4) + 4)
                pe.wait_ge(qh_done, ONE + ub + v)
                pe.wait_ge(ql_done, ONE + ub + v)
                for tc in range(TC):
                    m = pe.transpose(ps[0:QD, 5, tc * P:(tc + 1) * P], qs[:, (v // 4) % 2, tc, v % 4, :], ident[:])
                m.then_inc(q_tr, 1)

            def scores(ub, w, chunks):
                if 3 in chunks:
                    pe.wait_ge(qh_done, ONE + ub + w + 1)
                    pe.wait_ge(ql_done, ONE + ub + w + 1)
                    pe.wait_ge(s_red, ONE + (ub + w) * 4)
                else:
                    pe.wait_ge(s_red, ONE + (ub + w) * 4 + 1)
                for qc in chunks:
                    bank, off = SC_BANK[qc]
                    n = (qc + 1) * P
                    o = ps[:, bank, off:off + n]
                    q = slice(qc * P, (qc + 1) * P)
                    pe.matmul(o, q_hi[0:QD, w % 2, q], k_hi[0:QD, 0:n], start=True, stop=False)
                    pe.matmul(o, q_hi[0:QD, w % 2, q], k_lo[0:QD, 0:n], start=False, stop=False)
                    pe.matmul(o, q_lo[0:QD, w % 2, q], k_hi[0:QD, 0:n], start=False, stop=True).then_inc(s_done, 1)

            def batch(b, with_next):
                pe.wait_ge(qnT_done, b + 1)
                pe.wait_ge(kh_done, b + 1)
                pe.wait_ge(kl_done, b + 1)
                pe.wait_ge(in_done, ONE + b * IC)
                for p in range(4):
                    q_gen(b * H, p, 0)
                q_transpose(b * H, 0)
                pe.wait_ge(y_done, ONE + b * TC)
                scores(b * H, 0, SC_ORDER[:3])
                scores(b * H, 0, SC_ORDER[3:])
                for p in range(4, 7):
                    q_gen(b * H, p, 0)
                q_transpose(b * H, 1)
                scores(b * H, 1, SC_ORDER[:3])
                scores(b * H, 1, SC_ORDER[3:])
                q_transpose(b * H, 2)

                def step(ub, gb, gl, j, last):
                    g = j // 4
                    pe.wait_ge(p_done, ub + j + 1)
                    pe.wait_ge(pts_act, ONE + ub + j)
                    pe.wait_ge(pts_dve, ONE + ub + j)
                    for kc in range(TC):
                        for qc in range(kc, TC):
                            off = T_OFF[kc] + (qc - kc) * P
                            m = pe.transpose(ps[:, 2 + off // 512, off % 512:off % 512 + P],
                                             pr[:, j % 2, P_OFF[qc] + kc * P:P_OFF[qc] + (kc + 1) * P], ident[:])
                    m.then_inc(pt_done, 1)
                    if not (last and j + 7 >= 8):
                        q_gen(ub, j + 7, gl)
                    if not (last and j + 2 >= 8):
                        scores(ub, j + 2, SC_ORDER[:3])
                    if not (last and j + 3 >= 8):
                        q_transpose(ub, j + 3)
                    if j % 4 == 3:
                        pe.wait_ge(rb_done, ub + j + 1)
                        pe.wait_ge(ut_done, ONE + gb + g)
                        for qc in range(TC):
                            m = pe.transpose(ps[:, 6, qc * P:(qc + 1) * P],
                                             rb[:, g, qc].rearrange("p h c -> p (h c)"), ident[:])
                        m.then_inc(r_done, 1)
                    if not (last and j + 2 >= 8):
                        scores(ub, j + 2, SC_ORDER[3:])
                    if j % 4 == 3:
                        pe.wait_ge(pts_act, ONE + ub + j + 1)
                        pe.wait_ge(pts_dve, ONE + ub + j + 1)
                        pe.wait_ge(rsb_done, ONE + gb + g + 1)
                        for kc in range(TC):
                            for h in range(HG):
                                m = pe.matmul(ps[h * KVR:(h + 1) * KVR, 6, kc * P:], kt_sb[:, kc, 0:KVR],
                                              pts[:, h, T_OFF[kc]:T_OFF[kc] + S - kc * P],
                                              start=(kc == 0), stop=(kc == TC - 1))
                        m.then_inc(av_done, 1)
                steps(pe, b, step)

                def rows_t(t):
                    pe.wait_ge(xc_done, b * TC + t + 1)
                    if t >= 2:
                        pe.wait_ge(h2_done, b * TC + t - 1)
                    for k in range(KC):
                        m = pe.transpose(ps[:, 4 + t % 2, k * P:(k + 1) * P], xn[:, t, k * P:(k + 1) * P], ident[:])
                    m.then_inc(trc_done, 1)

                pe.wait_ge(ut_done, ONE + (b + 1) * G)
                for t in range(TC):
                    for g in range(G):
                        m = pe.matmul(ps[:, t, :], ut_sb[:, t, g * P:(g + 1) * P], g_sb[:, g, :],
                                      start=(g == 0), stop=(g == G - 1))
                    m.then_inc(op_done, 1)
                    if t >= 1:
                        rows_t(t - 1)
                rows_t(TC - 1)
                pe.wait_ge(h2hi_done, (b + 1) * TC)
                pe.wait_ge(h2lo_done, (b + 1) * TC)

                def down(ic):
                    M = rows_of(ic)
                    pe.wait_ge(ihi_done, b * IC + ic + 1)
                    pe.wait_ge(ilo_done, b * IC + ic + 1)
                    for t in range(TC):
                        for n, w in enumerate((i_hi, i_lo)):
                            m = pe.matmul(ps[:, t, :], w[0:M, ic % 2, t * P:(t + 1) * P], down_w[0:M, ic, :],
                                          start=(ic == 0 and n == 0), stop=(ic == IC - 1 and n == 1))
                        if ic == IC - 1:
                            m.then_inc(dn_done, 1)
                    if ic < IC - 1:
                        m.then_inc(dn_used, 1)

                order = ffn_order(with_next)
                for n, (kind, ic) in enumerate(order):
                    pair = 4 + 2 * (n % 2)
                    if n >= 2:
                        before, i = order[n - 2]
                        if before == "F":
                            pe.wait_ge(in_done, ONE + b * IC + i + 1)
                        elif before == "R":
                            pe.wait_ge(hT_done, (b + 1) * KC + 2 * i + 2)
                        elif before == "L":
                            pe.wait_ge(qa_done, b + 2)
                        else:
                            pe.wait_ge(qnT_done, b + 2)
                            pe.wait_ge(kl_done, b + 2)
                    if kind == "R":
                        pe_rows(pe, b + 1, ic, pair)
                        continue
                    if kind == "L":
                        pe_latents(pe, b + 1, pair)
                        continue
                    if kind == "T":
                        pe_latents_t(pe, b + 1, pair)
                        continue
                    M = rows_of(ic)
                    for w, bank, s_ in ((gate_w, pair, gate_ps), (up_w, pair + 1, up_ps)):
                        for k in range(KC):
                            for i, a in enumerate((h2_hi, h2_lo)):
                                m = pe.matmul(ps[0:M, bank, :], w[:, k, ic * P:ic * P + M], a[:, k, :],
                                              start=(k == 0 and i == 0), stop=(k == KC - 1 and i == 1))
                        m.then_inc(s_, 1)
                    if ic >= 1:
                        down(ic - 1)
                down(IC - 1)
            batches(pe, batch)

        @block.vector
        def _(dve):
            def q_rot(ub, p):
                dve.wait_ge(qg_done, ub + p + 1)
                if p >= 2:
                    dve.wait_ge(qs_done, (ub + p - 1) * 2)
                xq = ps[:, 7, HG * KVR:QW].rearrange("p (e h j) -> p e h j", e=2, h=HG)
                tc = p % 4
                dve.tensor_tensor(rot[:, p % 2, 0], xq,
                                  cos_sb[:, tc, :].unsqueeze(1).unsqueeze(1).broadcast_to((P, 2, HG, HALF)),
                                  ALU.mult).then_inc(qg_rot, 1)
                dve.tensor_tensor(rot[:, p % 2, 1], xq,
                                  sin_sb[:, tc].unsqueeze(2).broadcast_to((P, 2, HG, HALF)),
                                  ALU.mult).then_inc(qg_rot, 1)

            def q_low(ub, v):
                dve.wait_ge(qh_done, ONE + ub + v + 1)
                dve.tensor_tensor(q_lo[0:QD, v % 2, :], ps[0:QD, 5, :], q_hi[0:QD, v % 2, :].bitcast(F32),
                                  ALU.subtract).then_inc(ql_done, 1)

            def maxes(ub, w):
                if w >= 2:
                    dve.wait_ge(pt_done, ub + w - 1)
                for i, qc in enumerate(SC_ORDER):
                    if i != 2:
                        dve.wait_ge(s_done, ONE + (ub + w) * 4 + (1, 3, 3, 4)[i])
                        alone(dve)
                    bank, off = SC_BANK[qc]
                    n = (qc + 1) * P
                    dve.tensor_tensor_reduce(pr[:, w % 2, P_OFF[qc]:P_OFF[qc] + n], ps[:, bank, off:off + n],
                                             mask[:, S - n:S], 1.0, NEG, ALU.add, ALU.max,
                                             stat[:, 4 * (w % 2) + qc:4 * (w % 2) + qc + 1]).then_inc(s_red, 1)
                dve.wait_ge(s_red, ONE + (ub + w + 1) * 4)
                if w >= 2:
                    dve.wait_ge(p_done, ub + w - 1)
                dve.tensor_scalar(stat[:, 8 + 4 * (w % 2):12 + 4 * (w % 2)], stat[:, 4 * (w % 2):4 + 4 * (w % 2)],
                                  -SCALE, None, ALU.mult).then_inc(negm, 1)

            def batch(b, with_next):
                for p in range(4):
                    q_rot(b * H, p)
                q_low(b * H, 0)
                maxes(b * H, 0)
                for p in range(4, 7):
                    q_rot(b * H, p)
                q_low(b * H, 1)
                maxes(b * H, 1)
                q_low(b * H, 2)

                def step(ub, gb, gl, j, last):
                    g = j // 4
                    dve.wait_ge(pt_done, ub + j + 1)
                    dve.wait_ge(av_done, ONE + gb + g)
                    dve.tensor_copy(pts[:, j % 4, ACT_COLS:TRI], ps[:, 4, 0:TRI - ACT_COLS]).then_inc(pts_dve, 1)
                    dve.reciprocal(stat[:, 32 + 4 * (j % 4):36 + 4 * (j % 4)],
                                   stat[:, 16 + 4 * (j % 4):20 + 4 * (j % 4)]).then_inc(rs_done, 1)
                    if not (last and j + 7 >= 8):
                        q_rot(ub, j + 7)
                    if not (last and j + 2 >= 8):
                        maxes(ub, j + 2)
                    if not (last and j + 3 >= 8):
                        q_low(ub, j + 3)
                    if j % 4 == 3:
                        dve.wait_ge(y_out, ONE + b * (16 * TC))
                        dve.wait_ge(av_done, ONE + gb + g + 1)
                        dve.wait_ge(rsb_done, ONE + gb + g + 1)
                        dve.tensor_tensor(ut_sb[:, :, bass.ds((gl + g) * P, P)],
                                          ps[:, 6, :].rearrange("p (t n) -> p t n", t=TC),
                                          rsb[:].rearrange("p (t n) -> p t n", t=TC), ALU.mult).then_inc(ut_done, 1)
                steps(dve, b, step)

                n_c, link, linked = linker(dve, chain_c, b * N_CHAIN_C)
                dve.tensor_copy(mod_c[:], mod_all[:, 2:4, :, b]).then_inc(modc_done, 1)
                dve.wait_ge(ga_in, (b + 1) * 16)
                for t in range(TC):
                    dve.wait_ge(op_done, b * TC + t + 1)
                    link(dve.tensor_tensor(ut_sb[:, t, 0:D], ps[:, t, :], ga_sb[:], ALU.mult))
                    linked()
                    dve.tensor_tensor(ut_sb[:, t, 0:D], ut_sb[:, t, 0:D], x_sb[:, t, :], ALU.add).then_inc(x2_done, 1)
                    dve.wait_ge(x2_done, ONE + b * TC + t + 1)
                    link(dve.bn_stats(small_c[:, 0:6], ut_sb[:, t, 0:D]))
                    linked()
                    alone(dve)
                    link(dve.bn_aggr(small_c[:, 8:10], small_c[:, 0:6]))
                    linked()
                    rsqrt(dve, link, linked, small_c[:, 10:11], small_c[:, 9:10], small_c[:, 11:12],
                          small_c[:, 12:13], EPS_LN)
                    dve.tensor_scalar(xn[:, t, :], ut_sb[:, t, 0:D], small_c[:, 8:9], small_c[:, 10:11],
                                      ALU.subtract, ALU.mult).then_inc(xc_done, 1)
                    if t >= 1:
                        low(b, t - 1)
                low(b, TC - 1)
                pieces = dve_projections(dve, b + 1) if with_next else []
                for n, (kind, ic) in enumerate(ffn_order(with_next)):
                    pair = 4 + 2 * (n % 2)
                    if kind in "RL":
                        continue
                    if kind == "T":
                        dve_key_low(dve, b + 1, pair)
                        continue
                    M = rows_of(ic)
                    dve.wait_ge(gc_done, b * IC + ic + 1)
                    dve.wait_ge(up_ps, b * IC + ic + 1)
                    if ic >= 2:
                        dve.wait_ge(ihi_done, b * IC + ic - 1)
                        dve.wait_ge(ilo_done, b * IC + ic - 1)
                    dve.tensor_tensor(inter[0:M, ic % 2, :], ps[0:M, pair + 1, :], gcopy[0:M, ic % 2, :],
                                      ALU.mult).then_inc(in_done, 1)
                    dve.wait_ge(ihi_done, b * IC + ic + 1)
                    if ic >= 2:
                        dve.wait_ge(dn_used, b * (IC - 1) + ic - 1)
                    dve.tensor_tensor(i_lo[0:M, ic % 2, :], inter[0:M, ic % 2, :], i_hi[0:M, ic % 2, :].bitcast(F32),
                                      ALU.subtract).then_inc(ilo_done, 1)
                    if with_next and ic in DVE_AFTER:
                        pieces[DVE_AFTER[ic]]()
                dve.wait_ge(gb_in, (b + 1) * 16)
                for t in range(TC):
                    dve.wait_ge(dn_done, b * TC + t + 1)
                    link(dve.scalar_tensor_tensor(gcopy[:, t % 2, :], ps[:, t, :], bit[:, 25:26], gb_sb[:], ALU.mult,
                                                  ALU.mult))
                    linked()
                    dve.tensor_tensor(ut_sb[:, t, 0:D], gcopy[:, t % 2, :], ut_sb[:, t, 0:D],
                                      ALU.add).then_inc(y_done, 1)
                assert n_c[0] == N_CHAIN_C, n_c[0]

            def low(b, t):
                dve.wait_ge(h2hi_done, b * TC + t + 1)
                cols = slice(t * P, (t + 1) * P)
                dve.tensor_tensor(h2_lo[:, :, cols], h2[:, :, cols], h2_hi[:, :, cols].bitcast(F32),
                                  ALU.subtract).then_inc(h2lo_done, 1)
            batches(dve, batch)
    ctx.close()


def rope_tables():
    import math
    import numpy as np
    base, factor, orig = 10000.0, 128.0, 1024

    def corr_dim(r):
        return ROPE * math.log(orig / (r * 2 * math.pi)) / (2 * math.log(base))
    low = max(math.floor(corr_dim(32.0)), 0)
    high = min(math.ceil(corr_dim(1.0)), ROPE - 1)
    hi = high + 0.001 if low == high else float(high)
    ramp = np.clip((np.arange(HALF, dtype=np.float32) - low) / (hi - low), 0.0, 1.0)
    inv_freq_mask = 1.0 - ramp
    extra = 1.0 / base ** (np.arange(0, ROPE, 2, dtype=np.float32) / ROPE)
    inv_freq = extra / factor * (1.0 - inv_freq_mask) + extra * inv_freq_mask
    freqs = np.outer(np.arange(S, dtype=np.float32), inv_freq)
    cos, sin = np.cos(freqs).astype(np.float32), np.sin(freqs).astype(np.float32)
    return cos, np.ascontiguousarray(np.stack([sin, -sin], 1))


def kernel(L0_attn_x, L0_attn_wq_a, L0_attn_q_a_ln_w, L0_attn_wq_b, L0_attn_wkv_a, L0_attn_kv_a_ln_w, L0_attn_wkv_b,
           L0_attn_wo, L0_ffn_w_gate, L0_ffn_w_up, L0_ffn_w_down, L0_c, L0_wmod):
    import numpy as np
    import concourse.bacc as bacc
    from concourse.bass_utils import run_bass_kernel_spmd

    con = np.ascontiguousarray
    wq = np.asarray(L0_attn_wq_b).reshape(H, NOPE + ROPE, QR)
    wkv = np.asarray(L0_attn_wkv_b).reshape(H, NOPE + VD, KVR)
    kv_a = np.asarray(L0_attn_wkv_a)
    wa = con(np.concatenate([np.asarray(L0_attn_wq_a), kv_a[:KVR], kv_a[KVR::2], kv_a[KVR + 1::2]], 0).T)
    pe = wq[:, NOPE:].reshape(G, HG, HALF, 2, QR)
    cos, sin2 = rope_tables()
    arrays = {
        "x": con(L0_attn_x),
        "wa": wa,
        "wqn": con(wq[:, :NOPE].transpose(1, 0, 2)),
        "wkn": con(wkv[:, :NOPE].transpose(1, 0, 2)),
        "wqp": con(pe.transpose(4, 0, 3, 1, 2).reshape(QR, G, 2, HG * HALF)),
        "wv": con(wkv[:, NOPE:].transpose(1, 0, 2)),
        "wo": con(np.asarray(L0_attn_wo).reshape(D, H, VD).transpose(2, 1, 0)),
        "wg": con(np.asarray(L0_ffn_w_gate).T),
        "wu": con(np.asarray(L0_ffn_w_up).T),
        "wd": con(np.asarray(L0_ffn_w_down).T),
        "qln": con(np.asarray(L0_attn_q_a_ln_w).reshape(QR, 1)),
        "kvln": con(L0_attn_kv_a_ln_w),
        "cT": con(np.asarray(L0_c).T.reshape(KC, P, B).transpose(1, 0, 2).reshape(P, KC * B)),
        "wmod": con(L0_wmod),
        "cos": cos,
        "sin2": sin2,
    }
    nc = bacc.Bacc("TRN2", target_bir_lowering=False, num_devices=1)
    aps = {n: nc.dram_tensor(n, a.shape, F32, kind="ExternalInput").ap() for n, a in arrays.items()}
    out = nc.dram_tensor("out", (B, S, D), F32, kind="ExternalOutput").ap()
    mod_dram = nc.dram_tensor("mod_dram", (B, 6 * D), F32, kind="Internal").ap()
    adaln_block(nc, *aps.values(), out, mod_dram)
    r = run_bass_kernel_spmd(nc, [arrays], core_ids=[0])
    return r.results[0]["out"]
```

```python
from contextlib import ExitStack

import concourse.bass as bass
from concourse import mybir

F32 = mybir.dt.float32
F32R = mybir.dt.float32r
I32 = mybir.dt.int32
BF16 = mybir.dt.bfloat16
ALU = mybir.AluOpType
ACT = mybir.ActivationFunctionType
AX = mybir.AxisListType

P = 128
B, S, D = 4, 512, 512
H, NOPE, ROPE, VD, KVR, QR = 32, 64, 64, 128, 32, 128
HALF = ROPE // 2
I = 1376
TC = S // P
KC = D // P
IC = (I + P - 1) // P
HG = 4
G = H // HG
QD = KVR + ROPE
QW = HG * QD
QA = QR + KVR + ROPE
TRI = P * TC * (TC + 1) // 2
ONE = 1
NEG = -3.0e38
EPS_LN, EPS_RMS, EPS_BIT = 1e-5, 1e-6, 1e-5
MSCALE = 0.1 * 4.852030263919617 + 1.0
SCALE = (NOPE + ROPE) ** -0.5 * MSCALE * MSCALE

SC_ORDER = [3, 2, 0, 1]
SC_BANK = {3: (0, 0), 2: (1, 0), 0: (1, 384), 1: (0, 0)}
P_OFF = {3: 0, 2: 512, 0: 896, 1: 1024}
T_OFF = {0: 0, 1: 512, 3: 896, 2: 1024}
PTS_COLS = {("act", False): (S, TRI), ("dve", False): (0, S), ("act", True): (0, 2 * S), ("dve", True): (2 * S, TRI)}

DVE_AFTER = {1: (0, 1), 2: (2, 3), 5: (4,), 6: (5,)}
OUT_AT = {1: [(0, [0])], 2: [(0, [1])], 3: [(0, [2])], 4: [(0, [3])], 5: [(0, [4, 5]), (1, [0])],
          6: [(0, [6]), (1, [1, 2])], 7: [(1, [3, 4])]}
OUT_BANK = (7, 5, 0, 1)
UP_FIRST = 5
UP_AFTER = {0: (5,), 3: (6,), 4: (7, 8), 7: (9, 10)}
ROW_BANK = (4, 5, 2, 3)


def rows_of(ic):
    return min(P, I - ic * P)


def adaln_block(nc, x, wa, wqn, wkn, wqp, wv, wo, wg, wu, wd, qln, kvln, cT, wmod, cos, sin2, out, mod_dram):
    top = [(nc.sbuf_base + 31) // 32 * 32]

    def place(name, shape, dt=F32, at=None):
        size = 2 if dt is BF16 else 4
        for n in shape[1:]:
            size *= n
        off = top[0] if at is None else at
        t = nc.alloc_sbuf_tensor_at(name, list(shape), dt, offset=off)
        end = (off + size + 31) // 32 * 32
        assert end <= nc.sbuf_usable_end, name
        if at is None:
            top[0] = end
        return t, end

    ident, _ = place("ident", (P, P))
    ones, _ = place("ones", (P, P))
    mask, _ = place("mask", (P, S))
    cos_sb, _ = place("cos_sb", (P, TC, HALF))
    sin_sb, _ = place("sin_sb", (P, TC, 2, HALF))
    junk, e = place("junk", (P, IC * D // 4 // 2), at=top[0])
    below, _ = place("below", (P, 2, KC * I // 4), at=e)
    g_sb, _ = place("g_sb", (P, G, D))
    wq_sb, _ = place("wq_sb", (P, G * QW))
    wa_sb, _ = place("wa_sb", (P, KC, QA))
    kvln_sb, _ = place("kvln_sb", (P, KVR))
    qln_sb, _ = place("qln_sb", (P, 1))
    gate_raw, _ = place("gate_raw", (P, KC, I), at=top[0])
    gate_w, _ = place("gate_w", (P, KC, I), F32R)
    up_raw, _ = place("up_raw", (P, KC, I), at=top[0])
    up_w, _ = place("up_w", (P, KC, I), F32R)
    stage_c, _ = place("stage_c", (P, KC, 2 * D), at=top[0])
    down_raw, _ = place("down_raw", (P, IC, D), at=top[0])
    down_w, _ = place("down_w", (P, IC, D), F32R)
    bit, _ = place("bit", (P, 32))
    mod_all, _ = place("mod_all", (P, 4, KC, B))
    x_sb, _ = place("x_sb", (P, TC, D))
    wqn_t, _ = place("wqn_t", (NOPE, H, QR), at=top[0])
    ut_sb, _ = place("ut_sb", (P, TC, 2 * D))
    wkn_t, _ = place("wkn_t", (NOPE, H, KVR), at=top[0])
    ga_sb, _ = place("ga_sb", (P, D))
    gb_sb, _ = place("gb_sb", (P, D))
    mod_a, _ = place("mod_a", (P, 2, KC))
    mod_c, _ = place("mod_c", (P, 2, KC))
    qnT, _ = place("qnT", (P, S))
    kt_sb, _ = place("kt_sb", (P, TC, QD))
    k_hi, _ = place("k_hi", (P, S), F32R)
    k_lo, _ = place("k_lo", (P, S), F32R)
    small_a, _ = place("small_a", (P, 96))
    small_c, _ = place("small_c", (P, 96))
    shared = top[0]
    q_hi, e = place("q_hi", (P, 2, S), F32R, at=shared)
    q_lo, e = place("q_lo", (P, 2, S), F32R, at=e)
    rot, e = place("rot", (P, 2, 2, 2, HG, HALF), at=e)
    rb, e = place("rb", (P, 2, TC, HG, KVR), at=e)
    pr, e = place("pr", (P, 2, TRI), at=e)
    pts, e = place("pts", (P, HG, TRI), at=e)
    rsb, e = place("rsb", (P, S), at=e)
    qs, e = place("qs", (P, 2, TC, HG, QD), at=e)
    stat, e = place("stat", (P, 64), at=e)
    wo_g, e = place("wo_g", (P, HG, D), at=e)
    wv_g, e = place("wv_g", (P, HG, KVR), at=e)
    below_p, e = place("below_p", (P, S), BF16, at=e)
    xn, e = place("xn", (P, TC, D), at=shared)
    h2, e = place("h2", (P, KC, S), at=e)
    xn_a, hT = xn, h2
    stage, _ = place("stage", (P, 2, KC, 2 * D), at=e)
    h2_hi, e = place("h2_hi", (P, KC, S), F32R, at=e)
    h2_lo, e = place("h2_lo", (P, KC, S), F32R, at=e)
    gcopy, e = place("gcopy", (P, 2, S), at=e)
    inter, e = place("inter", (P, 2, S), at=e)
    i_hi, e = place("i_hi", (P, 2, S), F32R, at=e)
    i_lo, e = place("i_lo", (P, 2, S), F32R, at=e)
    qa_sb, e = place("qa_sb", (P, TC, QA), at=e)
    qtok, e = place("qtok", (P, TC, QR), at=e)
    scr, e = place("scr", (P, TC, QR), at=e)
    krot, e = place("krot", (P, 2, TC, 2, HALF), at=e)
    mrow, _ = place("mrow", (B, 6, D), at=e)
    c_t, ce_t, cs_t = small_c[:, 0:16], small_c[:, 16:32], small_c[:, 32:48]

    ctx = ExitStack()
    ps = ctx.enter_context(nc.psum_tensor("ps", [P, 8, 512], F32))

    def sem(name):
        return ctx.enter_context(nc.semaphore(name))

    su_w = [sem(f"su_w{i}") for i in range(3)]
    su_stage = [sem(f"su_stage{i}") for i in range(4)]
    su_const = sem("su_const")
    su_c = sem("su_c")
    su_qk = sem("su_qk")
    su_wqp = sem("su_wqp")
    su_wa = sem("su_wa")
    su_id = sem("su_id")
    su_exp = sem("su_exp")
    su_silu = sem("su_silu")
    su_modps = sem("su_modps")
    su_modsb = sem("su_modsb")
    su_gate = sem("su_gate")
    su_gst = sem("su_gst")
    su_mt = sem("su_mt")
    su_wqps = sem("su_wqps")
    su_wqsb = sem("su_wqsb")
    gw_in = sem("gw_in")
    gw_used = sem("gw_used")
    g_done = sem("g_done")
    below_done = sem("below_done")
    tern_done = sem("tern_done")
    up_below = sem("up_below")
    up_tern = sem("up_tern")
    su_sum = sem("su_sum")
    su_sumps = sem("su_sumps")
    su_bit = sem("su_bit")
    su_tern = sem("su_tern")
    su_pad = sem("su_pad")
    su_modall = sem("su_modall")

    waits_passed = sem("waits_passed")
    x_in = sem("x_in")
    ga_in = sem("ga_in")
    gb_in = sem("gb_in")
    moda_done = sem("moda_done")
    modc_done = sem("modc_done")
    x2_done = sem("x2_done")
    yp_done = sem("yp_done")
    y_done = sem("y_done")
    y_out = sem("y_out")
    chain_a = sem("chain_a")
    chain_c = sem("chain_c")
    xa_done = sem("xa_done")
    xc_done = sem("xc_done")
    tra_done = sem("tra_done")
    trc_done = sem("trc_done")
    hT_done = sem("hT_done")
    h2_done = sem("h2_done")
    qa_ps = sem("qa_ps")
    qa_done = sem("qa_done")
    tok_done = sem("tok_done")
    lat_tr = sem("lat_tr")
    qnT_done = sem("qnT_done")
    kh_done = sem("kh_done")
    kl_done = sem("kl_done")
    qg_done = sem("qg_done")
    qg_abs = sem("qg_abs")
    qg_rot = sem("qg_rot")
    qs_done = sem("qs_done")
    q_tr = sem("q_tr")
    qh_done = sem("qh_done")
    ql_done = sem("ql_done")
    s_done = sem("s_done")
    s_red = sem("s_red")
    negm = sem("negm")
    p_done = sem("p_done")
    pt_done = sem("pt_done")
    pts_act = sem("pts_act")
    pts_dve = sem("pts_dve")
    rs_done = sem("rs_done")
    rb_done = sem("rb_done")
    av_done = sem("av_done")
    r_done = sem("r_done")
    rsb_done = sem("rsb_done")
    ut_done = sem("ut_done")
    op_done = sem("op_done")
    h2hi_done = sem("h2hi_done")
    h2lo_done = sem("h2lo_done")
    gate_ps = sem("gate_ps")
    up_ps = sem("up_ps")
    gc_done = sem("gc_done")
    in_done = sem("in_done")
    ihi_done = sem("ihi_done")
    ilo_done = sem("ilo_done")
    dn_used = sem("dn_used")
    dn_done = sem("dn_done")

    from_one = [x2_done, y_done, yp_done, y_out, s_done, av_done, pts_act, pts_dve, rsb_done, qg_abs, qg_rot, qh_done,
                ql_done, s_red, ut_done, q_tr, in_done, gw_used, g_done, below_done, tern_done]

    def alone(eng):
        eng.sem_inc(waits_passed, 1)

    x_v = x.rearrange("b (t p) d -> b p t d", p=P)
    out_v = out.rearrange("b (t p) d -> b p t d", p=P)
    N_CHAIN_A, N_CHAIN_C = 50, 48

    def rsqrt(dve, link, linked, y, v, a, t, eps):
        link(dve.tensor_scalar(a, v, eps, None, ALU.add))
        linked()
        link(dve.tensor_scalar(t.bitcast(I32), a.bitcast(I32), 1, None, ALU.logical_shift_right))
        linked()
        link(dve.tensor_scalar(y.bitcast(I32), t.bitcast(I32), -1.0, float(0x5f3759df), ALU.mult, ALU.add))
        linked()
        for _ in range(3):
            link(dve.tensor_tensor(t, y, y, ALU.mult))
            linked()
            link(dve.scalar_tensor_tensor(t, t, -0.5, a, ALU.mult, ALU.mult))
            linked()
            link(dve.scalar_tensor_tensor(y, t, 1.5, y, ALU.add, ALU.mult))
            linked()

    def linker(eng, chain, base):
        n = [0]

        def link(ins):
            n[0] += 1
            ins.then_inc(chain, 1)

        def linked():
            eng.wait_ge(chain, base + n[0])
        return n, link, linked

    def pe_rows(pe, bb, half, pair):
        pe.wait_ge(xa_done, (bb + 1) * TC)
        for k in range(2 * half, 2 * half + 2):
            for t in range(TC):
                m = pe.transpose(ps[:, pair + k % 2, t * P:(t + 1) * P], xn_a[:, t, k * P:(k + 1) * P], ident[:])
            m.then_inc(tra_done, 1)

    def pe_latents(pe, bb, pair):
        pe.wait_ge(hT_done, (bb + 1) * KC)
        for t in range(TC):
            for k in range(KC):
                m = pe.matmul(ps[:, pair + t // 2, (t % 2) * 256:(t % 2) * 256 + QA], hT[:, k, t * P:(t + 1) * P],
                              wa_sb[:, k, :], start=(k == 0), stop=(k == KC - 1))
        m.then_inc(qa_ps, 1)

    def pe_latents_t(pe, bb, pair):
        pe.wait_ge(tok_done, (bb + 1) * 2)
        for t in range(TC):
            m = pe.transpose(ps[:, pair, t * P:(t + 1) * P], qtok[:, t, :], ident[:])
        m.then_inc(lat_tr, 1)
        for t in range(TC):
            m = pe.transpose(ps[0:QD, pair + 1, t * P:(t + 1) * P], kt_sb[:, t, :], ident[:])
        m.then_inc(lat_tr, 1)

    def act_rows(act, bb, half, pair):
        if half == 0:
            act.wait_ge(moda_done, bb + 1)
        for k in range(2 * half, 2 * half + 2):
            act.wait_ge(tra_done, bb * KC + k + 1)
            act.activation(hT[:, k, :], ps[:, pair + k % 2, :], ACT.Identity, bias=mod_a[:, 0, k:k + 1],
                           scale=mod_a[:, 1, k:k + 1]).then_inc(hT_done, 1)

    def act_latents(act, bb, pair):
        act.wait_ge(qa_ps, bb + 1)
        act.activation(qa_sb[:].rearrange("p (a t) n -> p a t n", a=2),
                       ps[:, pair:pair + 2, :].rearrange("p a (t n) -> p a t n", t=2)[:, :, :, 0:QA],
                       ACT.Copy).then_inc(qa_done, 1)

    def act_latents_t(act, bb, pair):
        act.wait_ge(lat_tr, bb * 2 + 1)
        act.activation(qnT[:], ps[:, pair, :], ACT.Copy, scale=qln_sb[:, 0:1]).then_inc(qnT_done, 1)
        act.wait_ge(lat_tr, bb * 2 + 2)
        act.activation(k_hi[0:QD, :], ps[0:QD, pair + 1, :], ACT.Copy).then_inc(kh_done, 1)

    def dve_projections(dve, bb):
        n, link, linked = linker(dve, chain_a, bb * N_CHAIN_A)
        mv = small_a[:, 24:32].rearrange("p (t e) -> p t e", e=2)

        def modulation():
            dve.tensor_copy(mod_a[:], mod_all[:, 0:2, :, bb]).then_inc(moda_done, 1)

        def statistics():
            dve.wait_ge(x_in, (bb + 1) * 16)
            for t in range(TC):
                link(dve.bn_stats(small_a[:, 6 * t:6 * t + 6], x_sb[:, t, :]))

        def root():
            linked()
            alone(dve)
            for t in range(TC):
                link(dve.bn_aggr(small_a[:, 24 + 2 * t:26 + 2 * t], small_a[:, 6 * t:6 * t + 6]))
            linked()
            rsqrt(dve, link, linked, small_a[:, 32:36], mv[:, :, 1], small_a[:, 64:68], small_a[:, 72:76], EPS_LN)

        def rows():
            for t in range(TC):
                dve.tensor_scalar(xn_a[:, t, :], x_sb[:, t, :], small_a[:, 24 + 2 * t:25 + 2 * t],
                                  small_a[:, 32 + t:33 + t], ALU.subtract, ALU.mult).then_inc(xa_done, 1)

        def norms():
            dve.wait_ge(qa_done, bb + 1)
            for t in range(TC):
                link(dve.tensor_tensor_reduce(scr[:, t, :], qa_sb[:, t, 0:QR], qa_sb[:, t, 0:QR], 1.0 / QR, 0.0,
                                              ALU.mult, ALU.add, small_a[:, 40 + t:41 + t]))
                link(dve.tensor_tensor_reduce(krot[:, 0, t, 0, :], qa_sb[:, t, QR:QR + KVR],
                                              qa_sb[:, t, QR:QR + KVR], 1.0 / KVR, 0.0,
                                              ALU.mult, ALU.add, small_a[:, 44 + t:45 + t]))
            linked()
            rsqrt(dve, link, linked, small_a[:, 48:56], small_a[:, 40:48], small_a[:, 64:72], small_a[:, 72:80],
                  EPS_RMS)

        def latents():
            for t in range(TC):
                link(dve.tensor_scalar(qtok[:, t, :], qa_sb[:, t, 0:QR], small_a[:, 48 + t:49 + t], None, ALU.mult))
                link(dve.scalar_tensor_tensor(kt_sb[:, t, 0:KVR], qa_sb[:, t, QR:QR + KVR],
                                              small_a[:, 52 + t:53 + t], kvln_sb[:], ALU.mult, ALU.mult))
            xk = qa_sb[:, :, QR + KVR:QA].rearrange("p t (e j) -> p t e j", e=2)
            link(dve.tensor_tensor(krot[:, 0], xk, cos_sb[:].unsqueeze(2).broadcast_to((P, TC, 2, HALF)), ALU.mult))
            link(dve.tensor_tensor(krot[:, 1], xk, sin_sb[:], ALU.mult))
            linked()
            dve.tensor_tensor(kt_sb[:, :, KVR:KVR + HALF], krot[:, 0, :, 0], krot[:, 1, :, 1],
                              ALU.add).then_inc(tok_done, 1)
            dve.tensor_tensor(kt_sb[:, :, KVR + HALF:QD], krot[:, 0, :, 1], krot[:, 1, :, 0],
                              ALU.add).then_inc(tok_done, 1)
            assert n[0] == N_CHAIN_A, n[0]

        return [modulation, statistics, root, rows, norms, latents]

    def dve_key_low(dve, bb, pair):
        dve.wait_ge(kh_done, bb + 1)
        dve.tensor_tensor(k_lo[0:QD, :], ps[0:QD, pair + 1, :], k_hi[0:QD, :].bitcast(F32),
                          ALU.subtract).then_inc(kl_done, 1)

    def ternary_up(dve, ic, under):
        M = rows_of(ic)
        raw, w = (a[:, :, ic * P:ic * P + M] for a in (up_raw, up_w))
        under = under[:, 0:KC * M].rearrange("p (k m) -> p k m", k=KC)
        if ic >= 1:
            dve.wait_ge(up_tern, ic)
        dve.tensor_scalar(under, raw, bit[:, 22:23], None, ALU.is_lt).then_inc(up_below, 1)
        dve.wait_ge(up_below, ic + 1)
        dve.scalar_tensor_tensor(w, raw, bit[:, 19:20], under, ALU.is_gt, ALU.subtract).then_inc(up_tern, 1)

    with nc.Block() as block:
        @block.sync
        def _(sp):
            for s_ in from_one:
                sp.sem_inc(s_, ONE)
            sp.dma_start(c_t, cT).then_inc(su_c, 16)
            wmod_v = wmod.rearrange("(k p) n -> p k n", p=P)
            sp.dma_start(stage[:, 0, :, 0:D], wmod_v[:, :, 0:D]).then_inc(su_stage[0], 16)
            sp.dma_start(stage[:, 0, :, D:2 * D], wmod_v[:, :, D:2 * D]).then_inc(su_stage[1], 16)
            sp.dma_start(stage[:, 1], wmod_v[:, :, 2 * D:4 * D]).then_inc(su_stage[2], 16)
            sp.dma_start(x_sb[:], x_v[0]).then_inc(x_in, 16)
            sp.dma_start(stage_c[:], wmod_v[:, :, 4 * D:6 * D]).then_inc(su_stage[3], 16)
            sp.dma_start(gate_raw[:], wg.rearrange("(k p) n -> p k n", p=P)).then_inc(su_w[0], 16)
            sp.dma_start(wqn_t[:], wqn).then_inc(su_qk, 16)
            sp.dma_start(wkn_t[:], wkn).then_inc(su_qk, 16)
            sp.dma_start(wa_sb[:], wa.rearrange("(k p) n -> p k n", p=P)).then_inc(su_wa, 16)
            sp.dma_start(cos_sb[:], cos.rearrange("(t p) j -> p t j", p=P)).then_inc(su_const, 16)
            sp.dma_start(sin_sb[:], sin2.rearrange("(t p) e j -> p t e j", p=P)).then_inc(su_const, 16)
            sp.dma_start(qln_sb[:], qln).then_inc(su_const, 16)
            sp.dma_start(kvln_sb[:], kvln.partition_broadcast(P)).then_inc(su_const, 16)
            sp.dma_start(up_raw[:], wu.rearrange("(k p) n -> p k n", p=P)).then_inc(su_w[1], 16)
            sp.dma_start(wq_sb[:].rearrange("p (g a n) -> p g a n", g=G, a=3)[:, :, 1:3, :], wqp).then_inc(su_wqp, 16)
            sp.wait_ge(su_modps, 6)
            sp.wait_ge(su_pad, 1)
            sp.dma_start(down_raw[:, 0:IC - 1, :],
                         wd[0:(IC - 1) * P, :].rearrange("(k p) n -> p k n", p=P)).then_inc(su_w[2], 16)
            sp.dma_start(down_raw[0:rows_of(IC - 1), IC - 1, :], wd[(IC - 1) * P:, :]).then_inc(su_w[2], 16)
            sp.wait_ge(su_gate, 4)
            sp.dma_start(mod_dram, mrow[:]).then_inc(su_gst, 16)
            sp.wait_ge(su_gst, 16)
            sp.wait_ge(su_wqp, 16)
            sp.wait_ge(su_wqps, 2)
            sp.dma_start(ga_sb[:], mod_dram[0, 2 * D:3 * D].partition_broadcast(P)).then_inc(ga_in, 16)
            sp.dma_start(gb_sb[:], mod_dram[0, 5 * D:6 * D].partition_broadcast(P)).then_inc(gb_in, 16)

        @block.gpsimd
        def _(pool):
            pool.memset(ident[:], 0.0).then_inc(su_id, 1)
            pool.memset(ones[:], 1.0).then_inc(su_id, 1)
            pool.memset(mask[:], 0.0).then_inc(su_id, 1)
            pool.memset(down_raw[:, IC - 1, :], 0.0).then_inc(su_pad, 1)
            pool.wait_ge(su_id, 3)
            pool.affine_select(out=ident[:], in_=ident[:], compare_op=ALU.not_equal, fill=1.0, base=0,
                               pattern=[[-1, P]], channel_multiplier=1).then_inc(su_id, 1)
            pool.affine_select(out=mask[:], in_=mask[:], compare_op=ALU.is_ge, fill=NEG, base=S - P,
                               pattern=[[-1, S]], channel_multiplier=1).then_inc(su_id, 1)

        @block.scalar
        def _(act):
            act.wait_ge(su_c, 16)
            act.activation(ce_t, c_t, ACT.Exp, scale=-1.0).then_inc(su_exp, 1)

            def sums(n, raw, need):
                act.wait_ge(su_w[n], need)
                flat = raw[:].rearrange("p a b -> p (a b)")
                q = flat.shape[1] // 4
                for i in range(4):
                    if 4 * n + i >= 1:
                        act.wait_ge(su_sum, 4 * n + i)
                    act.activation(junk[:].bitcast(BF16)[:, 0:q], flat[:, i * q:(i + 1) * q], ACT.Abs,
                                   accum_out=bit[:, 4 * n + i:4 * n + i + 1]).then_inc(su_sum, 1)

            def queries(i):
                act.wait_ge(su_wqps, i + 1)
                act.activation(wq_sb[:].rearrange("p (g a n) -> p g a n", g=G, a=3)[:, 4 * i:4 * i + 4, 0, :],
                               ps[:, 3 - i, :].rearrange("p (g n) -> p g n", g=4), ACT.Copy).then_inc(su_wqsb, 1)

            sums(0, gate_raw, 16)
            act_rows(act, 0, 0, 4)
            act_rows(act, 0, 1, 6)
            act_latents(act, 0, 4)
            queries(0)
            sums(1, up_raw, 16)
            act.wait_ge(su_const, 64)
            act_latents_t(act, 0, 6)
            sums(2, down_raw, 32)
            queries(1)

        @block.tensor
        def _(pe):
            def modulation(i):
                piece = stage_c[:] if i == 2 else stage[:, i]
                for n in range(2):
                    if i == 0 or n == 0:
                        pe.wait_ge(su_stage[n if i == 0 else i + 1], 16)
                    if 2 * i + n >= 2:
                        pe.wait_ge(su_modsb, 2 * i + n - 1)
                    for k in range(KC):
                        m = pe.matmul(ps[0:B, n, :], cs_t[:, k * B:(k + 1) * B], piece[:, k, n * D:(n + 1) * D],
                                      start=(k == 0), stop=(k == KC - 1))
                    m.then_inc(su_modps, 1)

            def weight_sum(n):
                pe.wait_ge(su_sum, 4 * n + 4)
                pe.matmul(ps[:, 0, n * 4:n * 4 + 4], ones[:], bit[:, 4 * n:4 * n + 4], start=True,
                          stop=True).then_inc(su_sumps, 1)

            pe.wait_ge(su_silu, 3)
            modulation(0)
            modulation(1)
            modulation(2)
            pe.wait_ge(su_id, 5)
            pe_rows(pe, 0, 0, 4)
            pe_rows(pe, 0, 1, 6)
            pe.wait_ge(su_modsb, 6)
            for n, a in enumerate((0, 1, 3, 4)):
                for k in range(KC):
                    i = (n * KC + k) * B
                    m = pe.transpose(ps[:, 2, i:i + B], mrow[:, a, k * P:(k + 1) * P], ident[0:B, 0:B])
            m.then_inc(su_mt, 1)

            def queries(i):
                for h in range(i * H // 4, (i + 1) * H // 4):
                    m = pe.matmul(ps[:, 3 - h // 16, (h % 16) * KVR:(h % 16 + 1) * KVR], wqn_t[:, h, :],
                                  wkn_t[:, h, :], start=True, stop=True)
                if i % 2 == 1:
                    m.then_inc(su_wqps, 1)

            pe.wait_ge(su_qk, 32)
            queries(0)
            weight_sum(0)
            pe.wait_ge(su_wa, 16)
            pe_latents(pe, 0, 4)
            queries(1)
            pe.wait_ge(su_modall, 1)
            queries(2)
            pe_latents_t(pe, 0, 6)
            queries(3)
            for n in (1, 2):
                pe.wait_ge(su_bit, 5 * n - 4)
                weight_sum(n)

        @block.vector
        def _(dve):
            dve.wait_ge(su_exp, 1)
            dve.tensor_scalar(ce_t, ce_t, 1.0, None, ALU.add).then_inc(su_silu, 1)
            dve.wait_ge(su_silu, 1)
            dve.reciprocal(cs_t, ce_t).then_inc(su_silu, 1)
            dve.wait_ge(su_silu, 2)
            dve.tensor_tensor(cs_t, cs_t, c_t, ALU.mult).then_inc(su_silu, 1)
            def modulation(i):
                dve.wait_ge(su_modps, i + 1)
                dve.tensor_copy(mrow[:, i, :], ps[0:B, i % 2, :]).then_inc(su_modsb, 1)

            def thresholds(n):
                dve.wait_ge(su_sumps, n + 1)
                dve.tensor_reduce(bit[:, 12 + n:13 + n], ps[:, 0, n * 4:n * 4 + 4], AX.X, ALU.add).then_inc(su_bit, 1)
                dve.wait_ge(su_bit, n * 5 + 1)
                dve.tensor_scalar(bit[:, 15 + n:16 + n], bit[:, 12 + n:13 + n], 1.0 / (I * D), None,
                                  ALU.mult).then_inc(su_bit, 1)
                dve.wait_ge(su_bit, n * 5 + 2)
                dve.tensor_scalar(bit[:, 18 + n:19 + n], bit[:, 15 + n:16 + n], EPS_BIT, 0.5, ALU.add,
                                  ALU.mult).then_inc(su_bit, 1)
                if n == 0:
                    dve.tensor_copy(bit[:, 24:25], bit[:, 15:16]).then_inc(su_bit, 1)
                else:
                    dve.tensor_tensor(bit[:, 24 + n:25 + n], bit[:, 23 + n:24 + n], bit[:, 15 + n:16 + n],
                                      ALU.mult).then_inc(su_bit, 1)
                dve.wait_ge(su_bit, n * 5 + 3)
                dve.tensor_scalar(bit[:, 21 + n:22 + n], bit[:, 18 + n:19 + n], -1.0, None, ALU.mult).then_inc(su_bit, 1)

            def ternary_gate():
                rf, wf = (a[:].rearrange("p a b -> p (a b)") for a in (gate_raw, gate_w))
                q = rf.shape[1] // 4
                for i in range(4):
                    sl = slice(i * q, (i + 1) * q)
                    if i >= 2:
                        dve.wait_ge(su_tern, 2 * i - 2)
                    dve.tensor_scalar(below[:, i % 2, :], rf[:, sl], bit[:, 21:22], None, ALU.is_lt).then_inc(su_tern, 1)
                    dve.wait_ge(su_tern, 2 * i + 1)
                    dve.scalar_tensor_tensor(wf[:, sl], rf[:, sl], bit[:, 18:19], below[:, i % 2, :],
                                             ALU.is_gt, ALU.subtract).then_inc(su_tern, 1)

            shifts, statistics, root, rows, norms, latents = dve_projections(dve, 0)
            for i in range(4):
                modulation(i)
                if i == 1:
                    statistics()
                    root()
            rows()
            for i in range(4, 6):
                modulation(i)
            dve.wait_ge(su_mt, 1)
            dve.tensor_copy(mod_all[:].rearrange("p a k b -> p (a k b)"), ps[:, 2, 0:4 * KC * B]).then_inc(su_modall, 1)
            dve.wait_ge(su_modall, 1)
            scales = mod_all[:].rearrange("p (e f) k b -> p e f (k b)", f=2)[:, :, 1, :]
            dve.tensor_scalar(scales, scales, 1.0, None, ALU.add).then_inc(su_modall, 1)
            dve.wait_ge(su_modall, 2)
            shifts()
            gates = mrow[:].rearrange("b (e f) n -> b e f n", e=2)[:, :, 2, :]
            size = mrow[:].rearrange("b (e f) n -> b e f n", e=2)[:, :, 0, :]
            dve.scalar_tensor_tensor(size, gates, -1.0, gates, ALU.mult, ALU.max).then_inc(su_gate, 1)
            dve.wait_ge(su_gate, 1)
            dve.tensor_scalar(gates, gates, 0.0, 2.0, ALU.is_ge, ALU.mult).then_inc(su_gate, 1)
            dve.wait_ge(su_gate, 2)
            dve.tensor_scalar(gates, gates, -1.0, None, ALU.add).then_inc(su_gate, 1)
            dve.wait_ge(su_gate, 3)
            dve.scalar_tensor_tensor(gates, size, 0.25, gates, ALU.max, ALU.mult).then_inc(su_gate, 1)
            thresholds(0)
            dve.wait_ge(su_bit, 5)
            ternary_gate()
            norms()
            dve.wait_ge(su_const, 64)
            latents()
            dve_key_low(dve, 0, 6)
            thresholds(1)
            dve.wait_ge(su_bit, 10)
            dve.wait_ge(su_tern, 8)
            for ic in range(UP_FIRST):
                ternary_up(dve, ic, below[:, 0])
            thresholds(2)
            dve.wait_ge(su_bit, 15)
            dve.wait_ge(up_tern, UP_FIRST)

    def low(eng, b, t):
        eng.wait_ge(h2hi_done, b * TC + t + 1)
        cols = slice(t * P, (t + 1) * P)
        eng.tensor_tensor(h2_lo[:, :, cols], h2[:, :, cols], h2_hi[:, :, cols].bitcast(F32),
                          ALU.subtract).then_inc(h2lo_done, 1)

    def steps(eng, b, step):
        with eng.Fori(0, H // 8 - 1) as it:
            for j in range(8):
                step(b * H + it * 8, b * G + it * 2, it * 2, j, False)
        it = H // 8 - 1
        for j in range(8):
            step(b * H + it * 8, b * G + it * 2, it * 2, j, True)

    def batches(eng, batch):
        batch(0, True, True)
        with eng.Fori(1, B - 1) as b:
            batch(b, True, False)
        batch(B - 1, False, False)

    START = [("Q", 0), ("Q", 1), ("Q", 2), ("X", 0), ("Q", 3), ("S", 0)]

    def ffn_order(with_next):
        if not with_next:
            return [("F", ic) for ic in range(IC)]
        return [("F", 0), ("F", 1), ("F", 2), ("F", 3), ("R", 0), ("R", 1), ("F", 4), ("L", 0), ("F", 5), ("F", 6),
                ("F", 7), ("T", 0), ("F", 8), ("Q", 0), ("Q", 1), ("F", 9), ("X", 0), ("Q", 2), ("F", 10), ("Q", 3),
                ("S", 0)]

    def parts_of(i):
        return range(2 * i, min(2 * i + 2, 7))

    with nc.Block() as block:
        @block.sync
        def _(sp):
            def batch(b, with_next, first):
                if first:
                    with sp.Fori(0, G) as g:
                        sp.wait_ge(gw_used, ONE + g)
                        alone(sp)
                        sp.dma_start(wo_g[:], wo[:, bass.ds(g * HG, HG), :]).then_inc(gw_in, 16)
                        sp.dma_start(wv_g[:], wv[:, bass.ds(g * HG, HG), :]).then_inc(gw_in, 16)
                if with_next:
                    sp.wait_ge(x2_done, ONE + (b + 1) * TC)
                    alone(sp)
                    sp.dma_start(x_sb[:], x_v[b + 1]).then_inc(x_in, 16)
                    sp.dma_start(ga_sb[:], mod_dram[b + 1, 2 * D:3 * D].partition_broadcast(P)).then_inc(ga_in, 16)
                for t in range(TC):
                    sp.wait_ge(y_done, ONE + b * TC + t + 1)
                    alone(sp)
                    sp.dma_start(out_v[b, :, t, :], ut_sb[:, t, 0:D]).then_inc(y_out, 16)
                if with_next:
                    sp.dma_start(gb_sb[:], mod_dram[b + 1, 5 * D:6 * D].partition_broadcast(P)).then_inc(gb_in, 16)
            batches(sp, batch)
            sp.wait_ge(y_out, ONE + B * 16 * TC)

        @block.gpsimd
        def _(pool):
            def rotate(pb, p, G_par, tc, first):
                pool.wait_ge(qg_rot, ONE + (pb + p + 1) * 2)
                if not first:
                    pool.wait_ge(q_tr, ONE + pb + 4 * (p // 4 - 1))
                r = rot[:, p % 2]
                o = qs[:, G_par, tc]
                pool.tensor_tensor(o[:, :, KVR:KVR + HALF], r[:, 0, 0], r[:, 1, 1], ALU.add).then_inc(qs_done, 1)
                pool.tensor_tensor(o[:, :, KVR + HALF:QD], r[:, 0, 1], r[:, 1, 0], ALU.add).then_inc(qs_done, 1)

            def batch(b, with_next, first):
                def step(ub, gb, gl, j, last):
                    pool.wait_ge(rs_done, ub + j + 1)
                    alone(pool)
                    pool.tensor_copy(rb[:, j // 4, :, j % 4, :],
                                     stat[:, 32 + 4 * (j % 4):36 + 4 * (j % 4)].unsqueeze(2).broadcast_to((P, TC, KVR))
                                     ).then_inc(rb_done, 1)
                    p = j + 7
                    if not (last and p >= 8):
                        rotate(ub, p, (p // 4) % 2, p % 4, False)
                steps(pool, b, step)
                for t in range(3):
                    low(pool, b, t)
                if with_next:
                    for p in range(7):
                        rotate((b + 1) * H, p, p // 4, p % 4, p < 4)
                for t in range(TC):
                    pool.wait_ge(yp_done, ONE + b * TC + t + 1)
                    pool.tensor_tensor(ut_sb[:, t, 0:D], ut_sb[:, t, D:2 * D], ut_sb[:, t, 0:D],
                                       ALU.add).then_inc(y_done, 1)

            for p in range(7):
                rotate(0, p, p // 4, p % 4, p < 4)
            batches(pool, batch)

        @block.scalar
        def _(act):
            def q_abs(ub, p, first, bank=7):
                act.wait_ge(qg_rot, ONE + (ub + p + 1) * 2)
                if not first:
                    act.wait_ge(q_tr, ONE + ub + 4 * (p // 4 - 1))
                act.activation(qs[:, (p // 4) % 2, p % 4, :, 0:KVR],
                               ps[:, bank, 0:HG * KVR].rearrange("p (h c) -> p h c", h=HG), ACT.Copy).then_inc(qg_abs, 1)

            def q_high(ub, v, bank=5):
                act.wait_ge(q_tr, ONE + ub + v + 1)
                if v >= 1:
                    act.wait_ge(s_done, ONE + (ub + v - 1) * 4)
                act.activation(q_hi[0:QD, v % 2, :], ps[0:QD, bank, :], ACT.Copy).then_inc(qh_done, 1)

            def exps(ub, x_):
                act.wait_ge(negm, ub + x_ + 1)
                for i, qc in enumerate(SC_ORDER):
                    n = (qc + 1) * P
                    pp = pr[:, x_ % 2, P_OFF[qc]:P_OFF[qc] + n]
                    m = act.activation(pp, pp, ACT.Exp, bias=stat[:, 8 + 4 * (x_ % 2) + qc:9 + 4 * (x_ % 2) + qc],
                                       scale=SCALE, accum_out=stat[:, 16 + 4 * (x_ % 4) + qc:17 + 4 * (x_ % 4) + qc])
                m.then_inc(p_done, 1)

            def batch(b, with_next, first):
                exps(b * H, 0)
                q_high(b * H, 2)

                def step(ub, gb, gl, j, last):
                    g = j // 4
                    if not (last and j + 1 >= 8):
                        exps(ub, j + 1)
                    act.wait_ge(pt_done, ub + j + 1)
                    act.wait_ge(av_done, ONE + gb + g)
                    lo, hi = PTS_COLS["act", first]
                    act.activation(pts[:, j % 4, lo:hi], ps[:, 2:5, :].rearrange("p a n -> p (a n)")[:, lo:hi],
                                   ACT.Copy).then_inc(pts_act, 1)
                    if j % 4 == 3:
                        act.wait_ge(r_done, gb + g + 1)
                        act.activation(rsb[:], ps[:, 6, :], ACT.Copy).then_inc(rsb_done, 1)
                    if not (last and j + 3 >= 8):
                        q_high(ub, j + 3)
                    if first and j % 4 == 1:
                        act.wait_ge(gw_used, ONE + gb + g + 1)
                        act.activation(g_sb[:, bass.ds(gl + g, 1), :], ps[:, 6:7, :], ACT.Copy).then_inc(g_done, 1)
                    if not (last and j + 7 >= 8):
                        q_abs(ub, j + 7, False)
                steps(act, b, step)

                act.wait_ge(modc_done, b + 1)
                for t in range(TC):
                    act.wait_ge(trc_done, b * TC + t + 1)
                    cols = slice(t * P, (t + 1) * P)
                    for k in range(KC):
                        m = act.activation(h2[:, k, cols], ps[:, ROW_BANK[t], k * P:(k + 1) * P], ACT.Identity,
                                           bias=mod_c[:, 0, k:k + 1], scale=mod_c[:, 1, k:k + 1])
                    m.then_inc(h2_done, 1)
                    act.wait_ge(h2_done, b * TC + t + 1)
                    act.activation(h2_hi[:, :, cols], h2[:, :, cols], ACT.Copy).then_inc(h2hi_done, 1)

                for n, (kind, ic) in enumerate(ffn_order(with_next)):
                    pair = 4 + 2 * (n % 2)
                    if kind != "F":
                        piece(b + 1, kind, ic, pair)
                        continue
                    M = rows_of(ic)
                    act.wait_ge(gate_ps, b * IC + ic + 1)
                    if ic >= 2:
                        act.wait_ge(in_done, ONE + b * IC + ic - 1)
                    act.activation(gcopy[0:M, ic % 2, :], ps[0:M, pair, :], ACT.Copy).then_inc(gc_done, 1)
                    act.wait_ge(in_done, ONE + b * IC + ic + 1)
                    if ic >= 2:
                        act.wait_ge(dn_used, b * (IC - 1) + ic - 1)
                    act.activation(i_hi[0:M, ic % 2, :], inter[0:M, ic % 2, :], ACT.Copy).then_inc(ihi_done, 1)

            def piece(bb, kind, i, pair):
                if kind == "R":
                    act_rows(act, bb, i, pair)
                elif kind == "L":
                    act_latents(act, bb, pair)
                elif kind == "T":
                    act_latents_t(act, bb, pair)
                elif kind == "Q":
                    for p in parts_of(i):
                        q_abs(bb * H, p, p < 4, pair + p % 2)
                elif kind == "X":
                    for v in range(2):
                        q_high(bb * H, v, pair + v)

            for n, (kind, i) in enumerate(START):
                piece(0, kind, i, 6 - 2 * (n % 2))
            batches(act, batch)

        @block.tensor
        def _(pe):
            def q_gen(ub, p, gl, bank=None):
                if bank is None:
                    bank = 7
                    pe.wait_ge(qg_abs, ONE + ub + p)
                    pe.wait_ge(qg_rot, ONE + (ub + p) * 2)
                tc = p % 4
                w = wq_sb[:, bass.ds((gl + p // 4) * QW, QW)]
                pe.matmul(ps[:, bank, 0:QW], qnT[:, tc * P:(tc + 1) * P], w, start=True,
                          stop=True).then_inc(qg_done, 1)

            def q_transpose(ub, v, bank=None):
                pe.wait_ge(qs_done, (ub + 4 * (v // 4) + 4) * 2)
                pe.wait_ge(qg_abs, ONE + ub + 4 * (v // 4) + 4)
                if bank is None:
                    bank = 5
                    pe.wait_ge(qh_done, ONE + ub + v)
                    pe.wait_ge(ql_done, ONE + ub + v)
                for tc in range(TC):
                    m = pe.transpose(ps[0:QD, bank, tc * P:(tc + 1) * P], qs[:, (v // 4) % 2, tc, v % 4, :], ident[:])
                m.then_inc(q_tr, 1)

            def scores(ub, w, chunks, base=0, again=True):
                if 3 in chunks:
                    pe.wait_ge(qh_done, ONE + ub + w + 1)
                    pe.wait_ge(ql_done, ONE + ub + w + 1)
                    if base == 0:
                        pe.wait_ge(s_red, ONE + (ub + w) * 4)
                elif again:
                    pe.wait_ge(s_red, ONE + (ub + w) * 4 + 1)
                for qc in chunks:
                    bank, off = SC_BANK[qc]
                    n = (qc + 1) * P
                    o = ps[:, base + bank, off:off + n]
                    q = slice(qc * P, (qc + 1) * P)
                    pe.matmul(o, q_hi[0:QD, w % 2, q], k_hi[0:QD, 0:n], start=True, stop=False)
                    pe.matmul(o, q_hi[0:QD, w % 2, q], k_lo[0:QD, 0:n], start=False, stop=False)
                    pe.matmul(o, q_lo[0:QD, w % 2, q], k_hi[0:QD, 0:n], start=False, stop=True).then_inc(s_done, 1)

            def piece(bb, kind, i, pair):
                if kind == "R":
                    pe_rows(pe, bb, i, pair)
                elif kind == "L":
                    pe_latents(pe, bb, pair)
                elif kind == "T":
                    pe_latents_t(pe, bb, pair)
                elif kind == "Q":
                    if i == 0:
                        pe.wait_ge(qnT_done, bb + 1)
                    for p in parts_of(i):
                        q_gen(bb * H, p, 0, pair + p % 2)
                elif kind == "X":
                    for v in range(2):
                        q_transpose(bb * H, v, pair + v)
                elif kind == "S":
                    pe.wait_ge(kh_done, bb + 1)
                    pe.wait_ge(kl_done, bb + 1)
                    scores(bb * H, 0, SC_ORDER[:3], pair)

            def free(bb, kind, i):
                if kind == "F":
                    pe.wait_ge(in_done, ONE + (bb - 1) * IC + i + 1)
                elif kind == "R":
                    pe.wait_ge(hT_done, bb * KC + 2 * i + 2)
                elif kind == "L":
                    pe.wait_ge(qa_done, bb + 1)
                elif kind == "T":
                    pe.wait_ge(qnT_done, bb + 1)
                    pe.wait_ge(kl_done, bb + 1)
                elif kind == "Q":
                    pe.wait_ge(qg_abs, ONE + bb * H + parts_of(i)[-1] + 1)
                elif kind == "X":
                    pe.wait_ge(qh_done, ONE + bb * H + 2)
                    pe.wait_ge(ql_done, ONE + bb * H + 2)

            def batch(b, with_next, first):
                pe.wait_ge(in_done, ONE + b * IC)
                pe.wait_ge(qg_abs, ONE + b * H + 7)
                scores(b * H, 1, SC_ORDER[:3], 6)
                pe.wait_ge(s_red, ONE + (b * H + 1) * 4)
                q_transpose(b * H, 2)
                if not first:
                    pe.wait_ge(yp_done, ONE + (b - 1) * TC + 1)
                scores(b * H, 1, SC_ORDER[3:], 0, False)
                pe.wait_ge(yp_done, ONE + b * TC)
                alone(pe)

                def out_rows(t, gs):
                    for g in gs:
                        m = pe.matmul(ps[:, OUT_BANK[t], :], ut_sb[:, t, g * P:(g + 1) * P], g_sb[:, g, :],
                                      start=(g == 0), stop=(g == G - 1))
                    if G - 1 in gs:
                        m.then_inc(op_done, 1)

                def step(ub, gb, gl, j, last):
                    g = j // 4
                    pe.wait_ge(p_done, ub + j + 1)
                    pe.wait_ge(pts_act, ONE + ub + j)
                    pe.wait_ge(pts_dve, ONE + ub + j)
                    for kc in range(TC):
                        for qc in range(kc, TC):
                            off = T_OFF[kc] + (qc - kc) * P
                            m = pe.transpose(ps[:, 2 + off // 512, off % 512:off % 512 + P],
                                             pr[:, j % 2, P_OFF[qc] + kc * P:P_OFF[qc] + (kc + 1) * P], ident[:])
                    m.then_inc(pt_done, 1)
                    if not (last and j + 7 >= 8):
                        if j == 0:
                            pe.wait_ge(s_red, ONE + (ub + 2) * 4)
                        q_gen(ub, j + 7, gl)
                    if not (last and j + 2 >= 8):
                        scores(ub, j + 2, SC_ORDER[:3])
                    if j % 4 == 3:
                        if first:
                            pe.wait_ge(g_done, ONE + gb + g + 1)
                        pe.wait_ge(rb_done, ub + j + 1)
                        pe.wait_ge(ut_done, ONE + gb + g)
                        for qc in range(TC):
                            m = pe.transpose(ps[:, 6, qc * P:(qc + 1) * P],
                                             rb[:, g, qc].rearrange("p h c -> p (h c)"), ident[:])
                        m.then_inc(r_done, 1)
                    if not (last and j + 3 >= 8):
                        q_transpose(ub, j + 3)
                    if first and j % 4 == 1:
                        pe.wait_ge(gw_in, (gb + g + 1) * 32)
                        pe.wait_ge(ut_done, ONE + gb + g)
                        for h in range(HG):
                            m = pe.matmul(ps[h * KVR:(h + 1) * KVR, 6, :], wv_g[:, h, :], wo_g[:, h, :],
                                          start=True, stop=True)
                        m.then_inc(gw_used, 1)
                    if not (last and j + 2 >= 8):
                        scores(ub, j + 2, SC_ORDER[3:])
                    if last and j == 1:
                        pe.wait_ge(qg_abs, ONE + ub + 8)
                        pe.wait_ge(qg_rot, ONE + (ub + 8) * 2)
                        pe.wait_ge(g_done, ONE + G - 2)
                        pe.wait_ge(ut_done, ONE + gb)
                    if last and j == 5:
                        pe.wait_ge(qh_done, ONE + ub + 8)
                        pe.wait_ge(ql_done, ONE + ub + 8)
                        pe.wait_ge(g_done, ONE + G - 1)
                        pe.wait_ge(ut_done, ONE + gb + 1)
                    if last and j == 7:
                        pe.wait_ge(s_red, ONE + (ub + 8) * 4)
                    if last:
                        for t, gs in OUT_AT.get(j, ()):
                            out_rows(t, gs)
                    if j % 4 == 3:
                        pe.wait_ge(pts_act, ONE + ub + j + 1)
                        pe.wait_ge(pts_dve, ONE + ub + j + 1)
                        pe.wait_ge(rsb_done, ONE + gb + g + 1)
                        for kc in range(TC):
                            for h in range(HG):
                                m = pe.matmul(ps[h * KVR:(h + 1) * KVR, 6, kc * P:], kt_sb[:, kc, 0:KVR],
                                              pts[:, h, T_OFF[kc]:T_OFF[kc] + S - kc * P],
                                              start=(kc == 0), stop=(kc == TC - 1))
                        m.then_inc(av_done, 1)
                steps(pe, b, step)

                def rows_t(t):
                    pe.wait_ge(xc_done, b * TC + t + 1)
                    for k in range(KC):
                        m = pe.transpose(ps[:, ROW_BANK[t], k * P:(k + 1) * P], xn[:, t, k * P:(k + 1) * P], ident[:])
                    m.then_inc(trc_done, 1)

                out_rows(1, range(5, G - 1))
                pe.wait_ge(g_done, ONE + G)
                pe.wait_ge(ut_done, ONE + (b + 1) * G)
                out_rows(0, [G - 1])
                out_rows(1, [G - 1])
                out_rows(2, range(G))
                out_rows(3, range(G // 2))
                rows_t(0)
                rows_t(1)
                out_rows(3, range(G // 2, G))
                rows_t(2)

                def gate_up(ic, pair, cols):
                    M = rows_of(ic)
                    for w, bank, s_ in ((gate_w, pair, gate_ps), (up_w, pair + 1, up_ps)):
                        for k in range(KC):
                            for i, a in enumerate((h2_hi, h2_lo)):
                                m = pe.matmul(ps[0:M, bank, cols], w[:, k, ic * P:ic * P + M], a[:, k, cols],
                                              start=(k == 0 and i == 0), stop=(k == KC - 1 and i == 1))
                        if cols.stop == S:
                            m.then_inc(s_, 1)

                pe.wait_ge(tern_done, ONE + H)
                pe.wait_ge(h2hi_done, b * TC + 2)
                pe.wait_ge(h2lo_done, b * TC + 2)
                gate_up(0, 4, slice(0, S // 2))
                gate_up(1, 6, slice(0, S // 2))
                rows_t(3)
                pe.wait_ge(h2hi_done, (b + 1) * TC)
                pe.wait_ge(h2lo_done, (b + 1) * TC)

                def down(ic, between=None):
                    M = rows_of(ic)
                    pe.wait_ge(ihi_done, b * IC + ic + 1)
                    pe.wait_ge(ilo_done, b * IC + ic + 1)
                    for t in range(TC):
                        for n, w in enumerate((i_hi, i_lo)):
                            m = pe.matmul(ps[:, t, :], w[0:M, ic % 2, t * P:(t + 1) * P], down_w[0:M, ic, :],
                                          start=(ic == 0 and n == 0), stop=(ic == IC - 1 and n == 1))
                        if ic == IC - 1:
                            m.then_inc(dn_done, 1)
                        if t == 1 and between is not None:
                            between()
                    if ic < IC - 1:
                        m.then_inc(dn_used, 1)

                order = ffn_order(with_next)
                for n, (kind, ic) in enumerate(order):
                    pair = 4 + 2 * (n % 2)
                    if n >= 2:
                        free(b + 1, *order[n - 2])
                    if kind == "S":
                        continue
                    if kind != "F":
                        piece(b + 1, kind, ic, pair)
                        continue
                    if first and ic >= UP_FIRST:
                        pe.wait_ge(up_tern, ic + 1)
                    gate_up(ic, pair, slice(S // 2 if ic < 2 else 0, S))
                    if ic >= 1:
                        down(ic - 1)
                if with_next:
                    piece(b + 1, "S", 0, pair)
                    down(IC - 1, lambda: scores((b + 1) * H, 0, SC_ORDER[3:], pair))
                else:
                    down(IC - 1)

            for n, (kind, i) in enumerate(START):
                if n >= 2:
                    free(0, *START[n - 2])
                piece(0, kind, i, 6 - 2 * (n % 2))
            scores(0, 0, SC_ORDER[3:], 4)
            batches(pe, batch)

        @block.vector
        def _(dve):
            def q_rot(ub, p, bank=7):
                dve.wait_ge(qg_done, ub + p + 1)
                if p >= 2:
                    dve.wait_ge(qs_done, (ub + p - 1) * 2)
                xq = ps[:, bank, HG * KVR:QW].rearrange("p (e h j) -> p e h j", e=2, h=HG)
                tc = p % 4
                dve.tensor_tensor(rot[:, p % 2, 0], xq,
                                  cos_sb[:, tc, :].unsqueeze(1).unsqueeze(1).broadcast_to((P, 2, HG, HALF)),
                                  ALU.mult).then_inc(qg_rot, 1)
                dve.tensor_tensor(rot[:, p % 2, 1], xq,
                                  sin_sb[:, tc].unsqueeze(2).broadcast_to((P, 2, HG, HALF)),
                                  ALU.mult).then_inc(qg_rot, 1)

            def q_low(ub, v, bank=5):
                dve.wait_ge(qh_done, ONE + ub + v + 1)
                dve.tensor_tensor(q_lo[0:QD, v % 2, :], ps[0:QD, bank, :], q_hi[0:QD, v % 2, :].bitcast(F32),
                                  ALU.subtract).then_inc(ql_done, 1)

            def maxes(ub, w, base=0, last_at=None, between=None):
                if w >= 2:
                    dve.wait_ge(pt_done, ub + w - 1)
                for i, qc in enumerate(SC_ORDER):
                    if i == 3 and between is not None:
                        between()
                    if i != 2:
                        dve.wait_ge(s_done, ONE + (ub + w) * 4 + (1, 3, 3, 4)[i])
                        alone(dve)
                    bank, off = SC_BANK[qc]
                    bank += base
                    if i == 3 and last_at is not None:
                        bank, off = last_at
                    n = (qc + 1) * P
                    dve.tensor_tensor_reduce(pr[:, w % 2, P_OFF[qc]:P_OFF[qc] + n], ps[:, bank, off:off + n],
                                             mask[:, S - n:S], 1.0, NEG, ALU.add, ALU.max,
                                             stat[:, 4 * (w % 2) + qc:4 * (w % 2) + qc + 1]).then_inc(s_red, 1)
                dve.wait_ge(s_red, ONE + (ub + w + 1) * 4)
                if w >= 2:
                    dve.wait_ge(p_done, ub + w - 1)
                dve.tensor_scalar(stat[:, 8 + 4 * (w % 2):12 + 4 * (w % 2)], stat[:, 4 * (w % 2):4 + 4 * (w % 2)],
                                  -SCALE, None, ALU.mult).then_inc(negm, 1)

            def batch(b, with_next, first):
                maxes(b * H, 1, 6, (0, 0))
                q_low(b * H, 2)

                def step(ub, gb, gl, j, last):
                    g = j // 4
                    dve.wait_ge(p_done, ub + j + 1)
                    if j >= 4:
                        dve.wait_ge(rb_done, ub + j - 3)
                    dve.reciprocal(stat[:, 32 + 4 * (j % 4):36 + 4 * (j % 4)],
                                   stat[:, 16 + 4 * (j % 4):20 + 4 * (j % 4)]).then_inc(rs_done, 1)
                    dve.wait_ge(pt_done, ub + j + 1)
                    dve.wait_ge(av_done, ONE + gb + g)
                    lo, hi = PTS_COLS["dve", first]
                    dve.tensor_copy(pts[:, j % 4, lo:hi],
                                    ps[:, 2:5, :].rearrange("p a n -> p (a n)")[:, lo:hi]).then_inc(pts_dve, 1)
                    if not (last and j + 7 >= 8):
                        q_rot(ub, j + 7)
                    if not (last and j + 2 >= 8):
                        maxes(ub, j + 2)
                    if not (last and j + 3 >= 8):
                        q_low(ub, j + 3)
                    if j % 4 == 3:
                        dve.wait_ge(y_out, ONE + b * (16 * TC))
                        dve.wait_ge(av_done, ONE + gb + g + 1)
                        dve.wait_ge(rsb_done, ONE + gb + g + 1)
                        dve.tensor_tensor(ut_sb[:, :, bass.ds((gl + g) * P, P)],
                                          ps[:, 6, :].rearrange("p (t n) -> p t n", t=TC),
                                          rsb[:].rearrange("p (t n) -> p t n", t=TC), ALU.mult).then_inc(ut_done, 1)
                    if first:
                        u, q = ub + j, IC * D // H
                        raw, w = (a[:].rearrange("p a b -> p (a b)")[:, bass.ds(u * q, q)] for a in (down_raw, down_w))
                        dve.wait_ge(tern_done, ONE + u)
                        dve.tensor_scalar(below_p[:, 0:q], raw, bit[:, 23:24], None, ALU.is_lt).then_inc(below_done, 1)
                        dve.wait_ge(below_done, ONE + u + 1)
                        dve.scalar_tensor_tensor(w, raw, bit[:, 20:21], below_p[:, 0:q], ALU.is_gt,
                                                 ALU.subtract).then_inc(tern_done, 1)
                steps(dve, b, step)

                n_c, link, linked = linker(dve, chain_c, b * N_CHAIN_C)
                dve.tensor_copy(mod_c[:], mod_all[:, 2:4, :, b]).then_inc(modc_done, 1)
                dve.wait_ge(ga_in, (b + 1) * 16)
                for ts in ((0, 1), (2,), (3,)):
                    w = len(ts)
                    for t in ts:
                        dve.wait_ge(op_done, b * TC + t + 1)
                        link(dve.tensor_tensor(ut_sb[:, t, 0:D], ps[:, OUT_BANK[t], :], ga_sb[:], ALU.mult))
                    linked()
                    for t in ts:
                        dve.tensor_tensor(ut_sb[:, t, 0:D], ut_sb[:, t, 0:D], x_sb[:, t, :],
                                          ALU.add).then_inc(x2_done, 1)
                    for i, t in enumerate(ts):
                        dve.wait_ge(x2_done, ONE + b * TC + t + 1)
                        link(dve.bn_stats(small_c[:, 6 * i:6 * i + 6], ut_sb[:, t, 0:D]))
                    linked()
                    alone(dve)
                    for i in range(w):
                        link(dve.bn_aggr(small_c[:, 12 + 2 * i:14 + 2 * i], small_c[:, 6 * i:6 * i + 6]))
                    linked()
                    var = small_c[:, 12:12 + 2 * w].rearrange("p (t e) -> p t e", e=2)[:, :, 1]
                    rsqrt(dve, link, linked, small_c[:, 16:16 + w], var, small_c[:, 20:20 + w],
                          small_c[:, 24:24 + w], EPS_LN)
                    for i, t in enumerate(ts):
                        dve.tensor_scalar(xn[:, t, :], ut_sb[:, t, 0:D], small_c[:, 12 + 2 * i:13 + 2 * i],
                                          small_c[:, 16 + i:17 + i], ALU.subtract, ALU.mult).then_inc(xc_done, 1)
                dve.wait_ge(h2lo_done, b * TC + 3)
                low(dve, b, 3)
                pieces = dve_projections(dve, b + 1) if with_next else []
                for n, (kind, ic) in enumerate(ffn_order(with_next)):
                    pair = 4 + 2 * (n % 2)
                    if kind == "S":
                        continue
                    if kind != "F":
                        piece(b + 1, kind, ic, pair)
                        continue
                    M = rows_of(ic)
                    dve.wait_ge(gc_done, b * IC + ic + 1)
                    dve.wait_ge(up_ps, b * IC + ic + 1)
                    if ic >= 2:
                        dve.wait_ge(ihi_done, b * IC + ic - 1)
                        dve.wait_ge(ilo_done, b * IC + ic - 1)
                    dve.tensor_tensor(inter[0:M, ic % 2, :], ps[0:M, pair + 1, :], gcopy[0:M, ic % 2, :],
                                      ALU.mult).then_inc(in_done, 1)
                    dve.wait_ge(ihi_done, b * IC + ic + 1)
                    if ic >= 2:
                        dve.wait_ge(dn_used, b * (IC - 1) + ic - 1)
                    dve.tensor_tensor(i_lo[0:M, ic % 2, :], inter[0:M, ic % 2, :], i_hi[0:M, ic % 2, :].bitcast(F32),
                                      ALU.subtract).then_inc(ilo_done, 1)
                    if first:
                        for later in UP_AFTER.get(ic, ()):
                            ternary_up(dve, later, below_p)
                    if with_next and ic in DVE_AFTER:
                        for i in DVE_AFTER[ic]:
                            pieces[i]()

                def out_row(t):
                    dve.wait_ge(dn_done, b * TC + t + 1)
                    dve.scalar_tensor_tensor(ut_sb[:, t, D:2 * D], ps[:, t, :], bit[:, 26:27], gb_sb[:], ALU.mult,
                                             ALU.mult).then_inc(yp_done, 1)

                dve.wait_ge(gb_in, (b + 1) * 16)
                if with_next:
                    maxes((b + 1) * H, 0, pair, between=lambda: out_row(0))
                else:
                    out_row(0)
                for t in range(1, TC):
                    out_row(t)
                assert n_c[0] == N_CHAIN_C, n_c[0]


            def piece(bb, kind, i, pair):
                if kind == "T":
                    dve_key_low(dve, bb, pair)
                elif kind == "Q":
                    for p in parts_of(i):
                        q_rot(bb * H, p, pair + p % 2)
                elif kind == "X":
                    for v in range(2):
                        q_low(bb * H, v, pair + v)
                elif kind == "S":
                    maxes(bb * H, 0, pair)

            for n, (kind, i) in enumerate(START):
                piece(0, kind, i, 6 - 2 * (n % 2))
            batches(dve, batch)
    ctx.close()


def rope_tables():
    import math
    import numpy as np
    base, factor, orig = 10000.0, 128.0, 1024

    def corr_dim(r):
        return ROPE * math.log(orig / (r * 2 * math.pi)) / (2 * math.log(base))
    low = max(math.floor(corr_dim(32.0)), 0)
    high = min(math.ceil(corr_dim(1.0)), ROPE - 1)
    hi = high + 0.001 if low == high else float(high)
    ramp = np.clip((np.arange(HALF, dtype=np.float32) - low) / (hi - low), 0.0, 1.0)
    inv_freq_mask = 1.0 - ramp
    extra = 1.0 / base ** (np.arange(0, ROPE, 2, dtype=np.float32) / ROPE)
    inv_freq = extra / factor * (1.0 - inv_freq_mask) + extra * inv_freq_mask
    freqs = np.outer(np.arange(S, dtype=np.float32), inv_freq)
    cos, sin = np.cos(freqs).astype(np.float32), np.sin(freqs).astype(np.float32)
    return cos, np.ascontiguousarray(np.stack([sin, -sin], 1))


def kernel(L0_attn_x, L0_attn_wq_a, L0_attn_q_a_ln_w, L0_attn_wq_b, L0_attn_wkv_a, L0_attn_kv_a_ln_w, L0_attn_wkv_b,
           L0_attn_wo, L0_ffn_w_gate, L0_ffn_w_up, L0_ffn_w_down, L0_c, L0_wmod):
    import numpy as np
    import concourse.bacc as bacc
    from concourse.bass_utils import run_bass_kernel_spmd

    con = np.ascontiguousarray
    wq = np.asarray(L0_attn_wq_b).reshape(H, NOPE + ROPE, QR)
    wkv = np.asarray(L0_attn_wkv_b).reshape(H, NOPE + VD, KVR)
    kv_a = np.asarray(L0_attn_wkv_a)
    wa = con(np.concatenate([np.asarray(L0_attn_wq_a), kv_a[:KVR], kv_a[KVR::2], kv_a[KVR + 1::2]], 0).T)
    pe = wq[:, NOPE:].reshape(G, HG, HALF, 2, QR)
    cos, sin2 = rope_tables()
    arrays = {
        "x": con(L0_attn_x),
        "wa": wa,
        "wqn": con(wq[:, :NOPE].transpose(1, 0, 2)),
        "wkn": con(wkv[:, :NOPE].transpose(1, 0, 2)),
        "wqp": con(pe.transpose(4, 0, 3, 1, 2).reshape(QR, G, 2, HG * HALF)),
        "wv": con(wkv[:, NOPE:].transpose(1, 0, 2)),
        "wo": con(np.asarray(L0_attn_wo).reshape(D, H, VD).transpose(2, 1, 0)),
        "wg": con(np.asarray(L0_ffn_w_gate).T),
        "wu": con(np.asarray(L0_ffn_w_up).T),
        "wd": con(np.asarray(L0_ffn_w_down).T),
        "qln": con(np.asarray(L0_attn_q_a_ln_w).reshape(QR, 1)),
        "kvln": con(L0_attn_kv_a_ln_w),
        "cT": con(np.asarray(L0_c).T.reshape(KC, P, B).transpose(1, 0, 2).reshape(P, KC * B)),
        "wmod": con(L0_wmod),
        "cos": cos,
        "sin2": sin2,
    }
    nc = bacc.Bacc("TRN2", target_bir_lowering=False, num_devices=1)
    aps = {n: nc.dram_tensor(n, a.shape, F32, kind="ExternalInput").ap() for n, a in arrays.items()}
    out = nc.dram_tensor("out", (B, S, D), F32, kind="ExternalOutput").ap()
    mod_dram = nc.dram_tensor("mod_dram", (B, 6 * D), F32, kind="Internal").ap()
    adaln_block(nc, *aps.values(), out, mod_dram)
    r = run_bass_kernel_spmd(nc, [arrays], core_ids=[0])
    return r.results[0]["out"]
```
